# Optimizing a Trainium2 kernel written in Bass

```python
import numpy as np
import jax
import jax.numpy as jnp

def _softmax(x, axis=-1):
    return jax.nn.softmax(x, axis=axis)

def _gelu(x):
    return jax.nn.gelu(x, approximate=True)

def _silu(x):
    return jax.nn.silu(x)

def _sigmoid(x):
    return jax.nn.sigmoid(x)

def _layernorm(x, axis=-1, eps=1e-05):
    m = jnp.mean(x, axis=axis, keepdims=True)
    v = jnp.var(x, axis=axis, keepdims=True)
    return (x - m) / jnp.sqrt(v + eps)

def _scatter_add(tgt, idx, src, axis=0):
    return tgt.at[idx].add(src)

def _segment_sum(src, seg, n):
    return jax.ops.segment_sum(src, seg, n)
kernel_name = 'mk_seq_preln_d1_jaxref_r8_d2c7a4'

def setup_inputs(seed: int=0):
    np.random.seed(seed)
    _w = jnp.asarray

    def _L0_attn_setup():
        import jax, jax.numpy as jnp
        import numpy as np
        key = jax.random.key(seed)
        kx, kt = jax.random.split(key)
        b, n, d = (4, 512, 128)
        x = jax.random.normal(kx, (b, n, d), dtype=jnp.float32)
        t = jax.random.normal(kt, (n, d), dtype=jnp.float32)
        return {'x': x, 't': t}
    _L0_attn_in = _L0_attn_setup()

    def _L0_ffn_setup():
        import jax, jax.numpy as jnp
        import numpy as np
        D = 128
        N_EXP = 8
        TOP_K = 1
        key = jax.random.key(seed)
        ks = jax.random.split(key, 7)
        s = 0.02
        return {'x': jax.random.normal(ks[0], (4, 256, D), jnp.float32), 'gate_w': jax.random.normal(ks[1], (D, N_EXP), jnp.float32) * s, 'gate_b': jnp.zeros((N_EXP,), jnp.float32), 'w1': jax.random.normal(ks[2], (N_EXP, D, 4 * D), jnp.float32) * s, 'b1': jnp.zeros((N_EXP, 4 * D), jnp.float32), 'w2': jax.random.normal(ks[3], (N_EXP, 4 * D, D), jnp.float32) * s, 'b2': jnp.zeros((N_EXP, D), jnp.float32)}
    _L0_ffn_in = _L0_ffn_setup()
    _d = {'L0_attn_x': _L0_attn_in['x'], 'L0_attn_t': _L0_attn_in['t'], 'L0_ffn_gate_w': _L0_ffn_in['gate_w'], 'L0_ffn_gate_b': _L0_ffn_in['gate_b'], 'L0_ffn_w1': _L0_ffn_in['w1'], 'L0_ffn_b1': _L0_ffn_in['b1'], 'L0_ffn_w2': _L0_ffn_in['w2'], 'L0_ffn_b2': _L0_ffn_in['b2']}
    _x0 = _d['L0_attn_x']
    _d['L0_attn_x'] = jax.random.normal(jax.random.fold_in(jax.random.key(seed), 1), (4, 512, 128), dtype=_x0.dtype)
    del _x0
    return _d

def reference(L0_attn_x, L0_attn_t, L0_ffn_gate_w, L0_ffn_gate_b, L0_ffn_w1, L0_ffn_b1, L0_ffn_w2, L0_ffn_b2):

    def _L0_attn_ref(x, t):
        import jax, jax.numpy as jnp
        import numpy as np
        b, n, d = x.shape
        L = 2 * n
        xf = jnp.fft.rfft(x.astype(jnp.float32), n=L, axis=1)
        tf = jnp.fft.rfft(t.astype(jnp.float32), n=L, axis=0)
        y = jnp.fft.irfft(xf * tf[None], n=L, axis=1)[:, :n, :]
        return y.astype(x.dtype)

    def _L0_ffn_ref(x, gate_w, gate_b, w1, b1, w2, b2):
        import jax, jax.numpy as jnp
        import numpy as np
        D = 128
        N_EXP = 8
        TOP_K = 1
        b, s, d = x.shape
        xf = x.reshape(-1, d)
        logits = xf @ gate_w + gate_b
        pb = jax.nn.softmax(logits, axis=-1)
        _, idx = jax.lax.top_k(pb, TOP_K)
        sel = jnp.any(idx[:, :, None] == jnp.arange(N_EXP)[None, None, :], axis=1)
        weights = pb * sel

        def expert_step(acc, params):
            w1e, b1e, w2e, b2e, wgt = params
            h = jax.nn.gelu(xf @ w1e + b1e, approximate=False)
            y = h @ w2e + b2e
            return (acc + wgt[:, None] * y, None)
        out0 = jnp.zeros_like(xf)
        out, _ = jax.lax.scan(expert_step, out0, (w1, b1, w2, b2, weights.T))
        return out.reshape(b, s, d)
    x = L0_attn_x
    x = x + _L0_attn_ref(_layernorm(x, axis=-1), L0_attn_t)
    x = x + _L0_ffn_ref(_layernorm(x, axis=-1), L0_ffn_gate_w, L0_ffn_gate_b, L0_ffn_w1, L0_ffn_b1, L0_ffn_w2, L0_ffn_b2)
    return x

_drawn_inputs = setup_inputs


def setup_inputs(seed=0):
    import zlib

    import numpy as np

    out = dict(_drawn_inputs(seed))
    spreads = {'L0_ffn_gate_b': (0.0, 0.8), 'L0_ffn_b1': (0.0, 0.8), 'L0_ffn_b2': (0.0, 2.0)}
    factors = {'L0_ffn_gate_w': 8.0, 'L0_ffn_w1': 8.0, 'L0_ffn_w2': 8.0}
    for name, (base, spread) in spreads.items():
        noise = np.random.default_rng([zlib.crc32(name.encode()), seed]).standard_normal(out[name].shape)
        drawn = base * np.exp(spread * noise) if base else spread * noise
        out[name] = jnp.asarray(drawn.astype(out[name].dtype))
    for name, factor in factors.items():
        out[name] = (out[name] * factor).astype(out[name].dtype)
    return out
```

```python
from contextlib import ExitStack

import concourse.bass as bass
from concourse import mybir

P = 128
ALU = mybir.AluOpType
ACT = mybir.ActivationFunctionType
F32 = mybir.dt.float32
I32 = mybir.dt.int32
U32 = mybir.dt.uint32
AX_X = mybir.AxisListType.X

B, N, D = 4, 512, 128
BLK = 2
S = N // BLK // P
KT = N // 2 // P
G = BLK * B * S
NE = 8
FF = 512
C = FF // P
TILES = G + NE - 1
EPS = 1e-5
ROW = D + 4
RSTD, NMR, WGT, TOK = D, D + 1, D + 2, D + 3
FIRST = 7

M_ID, M_TRI, M_ALT, M_PICK, M_CARRY, M_IOTA = 0, P, 2 * P, 2 * P + 2, 3 * P + 2, 4 * P + 2
M_COLS = M_IOTA + TILES * NE


def build(nc, x, t, gate_w, gate_b, w1, b1, w2, b2, fwd, inv, misc, tok, out):
    with ExitStack() as ctx:
        def sb(name, shape, dt=F32):
            return ctx.enter_context(nc.sbuf_tensor(name, shape, dt))

        def sem(name):
            return ctx.enter_context(nc.semaphore(name))

        x_sb = sb("x_sb", [P, BLK, B, S, D])
        xn = sb("xn", [P, BLK, B, S, D])
        t_sb = sb("t_sb", [P, BLK, S, D])
        fwd_sb = sb("fwd_sb", [P, S, KT, 2, P])
        inv_sb = sb("inv_sb", [P, KT, 2, S, P])
        misc_sb = sb("misc_sb", [P, M_COLS])
        ones_sb = sb("ones_sb", [P, P])
        tok_sb = sb("tok_sb", [P, G], I32)
        gw_sb = sb("gw_sb", [P, NE])
        gb_sb = sb("gb_sb", [P, NE])
        w1_sb = sb("w1_sb", [P, NE, FF])
        w2_sb = sb("w2_sb", [P, NE, C, D])
        b1_sb = sb("b1_sb", [P, NE, C])
        b2_sb = sb("b2_sb", [P, NE, D])
        st = sb("st", [P, G, 6])
        mv = sb("mv", [P, G, 2])
        var = sb("var", [P, G])
        half = sb("half", [P, G])
        rstd = sb("rstd", [P, G])
        nmr = sb("nmr", [P, G])
        ts = sb("ts", [P, KT, BLK, 2, D])
        k0i = sb("k0i", [P, KT, 2, D])
        k1r = sb("k1r", [P, KT, D])
        k1i = sb("k1i", [P, KT, 2, D])
        pr = sb("pr", [P, 4, 2, N])
        ya = sb("ya", [P, KT, BLK, 2, N])
        rows = sb("rows", [P, BLK, B, S, ROW])
        xT = sb("xT", [P, G, P])
        lg = sb("lg", [P, NE, G])
        df = sb("df", [P, NE, G])
        ex = sb("ex", [P, NE, G])
        sc = sb("sc", [P, NE, G])
        oh = sb("oh", [P, NE, G])
        inc = sb("inc", [P, NE, G])
        pos3 = sb("pos3", [P, NE, G])
        m16 = sb("m16", [P, 4, G])
        cnt = sb("cnt", [P, 2, NE], I32)
        ends = sb("ends", [P, 2, NE])
        posi = sb("posi", [P, 4, G], I32)
        slot = sb("slot", [P, G], U32)
        cmp = sb("cmp", [P, TILES, NE])
        ecnt = sb("ecnt", [P, TILES])
        eidx = sb("eidx", [P, TILES + 1], I32)
        xs = sb("xs", [P, TILES, ROW])
        xsn = sb("xsn", [P, 2, D])
        xsT = sb("xsT", [P, 2, P])
        wst = sb("wst", [P, 2, C, P])
        hT = sb("hT", [P, 2, C, P])
        yb = sb("yb", [P, 2, D])
        ob = sb("ob", [P, 2, D])
        ib = sb("ib", [P, 2, 1], U32)
        warm = sb("warm", [P, 2])
        ps = ctx.enter_context(nc.psum_tensor("ps", [P, 8, 512], F32))
        scratch = nc.dram_tensor("scratch", [P * TILES, ROW], F32)

        x_in = [[sem(f"x_in{k}{h}") for h in range(2)] for k in range(BLK)]
        t_in, fwd_in, inv_in, misc_in, tok_in = (sem(n) for n in ("t_in", "fwd_in", "inv_in", "misc_in", "tok_in"))
        gate_in, w1_in, w2_in, b1_in, b2_in = (sem(n) for n in ("gate_in", "w1_in", "w2_in", "b1_in", "b2_in"))
        dve_step = sem("dve_step")
        pool_step = sem("pool_step")
        ones_set = sem("ones_set")
        half_set = sem("half_set")
        blank_set, blank_out = sem("blank_set"), sem("blank_out")
        var_done, rstd_done, nmr_done = sem("var_done"), sem("rstd_done"), sem("nmr_done")
        xn_done = sem("xn_done")
        t_spec, t_copied, k0_done = sem("t_spec"), sem("t_copied"), sem("k0_done")
        x_spec, y_spec, y_conv = sem("x_spec"), sem("y_spec"), sem("y_conv")
        tok_set, row_done = sem("tok_set"), sem("row_done")
        xt_psum, xt_done, logits = sem("xt_psum"), sem("xt_done"), sem("logits")
        df_done, ex_done, oh_done, counted = sem("df_done"), sem("ex_done"), sem("oh_done"), sem("counted")
        eidx_done, slot_done, rows_out = sem("eidx_done"), sem("slot_done"), sem("rows_out")
        xs_in = [sem("xs_in0"), sem("xs_in1")]
        xsn_done, xsT_psum, xsT_done = sem("xsn_done"), sem("xsT_psum"), sem("xsT_done")
        wst_done, h_psum, h_done = sem("wst_done"), sem("h_psum"), sem("h_done")
        y_psum, yb_done, o_done = sem("y_psum"), sem("yb_done"), sem("o_done")
        o_out = [sem("o_out0"), sem("o_out1")]

        xg = x_sb.rearrange("p k b s d -> p (k b s) d")
        xng = xn.rearrange("p k b s d -> p (k b s) d")
        rg = rows.rearrange("p k b s r -> p (k b s) r")
        ident = misc_sb[:, M_ID:M_ID + P]
        tri = misc_sb[:, M_TRI:M_TRI + P]
        alt, nalt = misc_sb[:, M_ALT:M_ALT + 1], misc_sb[:, M_ALT + 1:M_ALT + 2]
        pick = misc_sb[:, M_PICK:M_PICK + P]
        carry = misc_sb[:, M_CARRY:M_CARRY + P]
        iota = misc_sb[0:1, M_IOTA:M_COLS].rearrange("p (t e) -> p t e", e=NE)
        lg_ps = ps[:, 0, 0:P]
        rank_ps, tot_ps = ps[:, 1, 0:P], ps[:, 2, 0:P]

        def flat(a):
            return a.rearrange("p e g -> p (e g)")

        def by_group(a):
            return a.rearrange("p e g -> p g e")

        def all_e(a):
            return a.unsqueeze(1).to_broadcast([P, NE, G])

        def tiles(eng, step, first, last):
            lo, hi = 4, 20
            for t in range(first, lo):
                step(t, t % 2)
            with eng.Fori(lo // 2, hi // 2) as i:
                step(i * 2, 0)
                step(i * 2 + 1, 1)
            for t in range(hi, last + 1):
                step(t, t % 2)

        def plain(t):
            return isinstance(t, int)

        block = ctx.enter_context(nc.Block())

        @block.sync
        def _(sp):
            xv = x.rearrange("b (k p s) d -> k p b (s d)", k=BLK, s=S)
            for k in range(BLK):
                for h in range(2):
                    sp.dma_start(x_sb[:, k, 2 * h:2 * h + 2].rearrange("p b s d -> p b (s d)"),
                                 xv[k, :, 2 * h:2 * h + 2, :]).then_inc(x_in[k][h], 16)
            sp.dma_start(inv_sb.rearrange("p a b c d -> p (a b c d)"), inv).then_inc(inv_in, 16)
            sp.dma_start(w1_sb[:], w1.rearrange("e d f -> d e f")).then_inc(w1_in, 16)
            sp.dma_start(w2_sb.rearrange("p e c d -> p e (c d)"),
                         w2.rearrange("e (p c) d -> p e (c d)", c=C)).then_inc(w2_in, 16)
            sp.wait_ge(blank_set, 2)
            sp.dma_start(scratch.rearrange("(p t) r -> p (t r)", t=TILES),
                         xs.rearrange("p t r -> p (t r)")).then_inc(blank_out, 16)
            sp.wait_ge(rows_out, 16 * G)
            sv = scratch.rearrange("(p t) r -> p t r", t=TILES)
            for n, (a, b) in enumerate(((0, FIRST), (FIRST, TILES))):
                sp.dma_start(xs[:, a:b, :].rearrange("p t r -> p (t r)"),
                             sv[:, a:b, :].rearrange("p t r -> p (t r)")).then_inc(xs_in[n], 16)

        @block.scalar
        def _(act):
            act.dma_start(t_sb.rearrange("p k s d -> p k (s d)"),
                          t.rearrange("(k p s) d -> p k (s d)", k=BLK, s=S)).then_inc(t_in, 16)
            act.dma_start(fwd_sb.rearrange("p a b c d -> p (a b c d)"), fwd).then_inc(fwd_in, 16)
            act.dma_start(misc_sb[:], misc).then_inc(misc_in, 16)
            act.dma_start(tok_sb[:], tok).then_inc(tok_in, 16)
            act.dma_start(gw_sb[:], gate_w).then_inc(gate_in, 16)
            act.dma_start(gb_sb[:], gate_b.partition_broadcast(P)).then_inc(gate_in, 16)
            act.dma_start(b1_sb[:], b1.rearrange("e (p c) -> p e c", c=C)).then_inc(b1_in, 16)
            act.dma_start(b2_sb.rearrange("p e d -> p (e d)"),
                          b2.rearrange("e d -> (e d)").partition_broadcast(P)).then_inc(b2_in, 16)
            for kt in range(KT):
                act.wait_ge(t_spec, kt + 1)
                nc.scalar.activation(ts[:, kt].rearrange("p k r d -> p (k r d)"), ps[:, 6 + kt, :],
                                     ACT.Copy).then_inc(t_copied, 1)
            for g in range(G):
                act.wait_ge(nmr_done, g // (G // BLK) + 1)
                nc.scalar.activation(xng[:, g, :], xg[:, g, :], ACT.Identity, bias=nmr[:, g:g + 1],
                                     scale=rstd[:, g:g + 1]).then_inc(xn_done, 1)
            act.wait_ge(x_spec, 2 * BLK * KT)
            for g in range(G):
                act.wait_ge(nmr_done, BLK + g // (G // BLK) + 1)
                nc.scalar.activation(xng[:, g, :], rg[:, g, 0:D], ACT.Identity, bias=nmr[:, g:g + 1],
                                     scale=rstd[:, g:g + 1]).then_inc(xn_done, 1)
                if g % 4 == 3:
                    q = g // 4
                    if q >= 1:
                        act.wait_ge(xt_psum, q)
                        nc.scalar.activation(xT[:, 4 * q - 4:4 * q, :].rearrange("p g d -> p (g d)"),
                                             ps[:, 3 + q, :], ACT.Copy).then_inc(xt_done, 1)
            act.wait_ge(xt_psum, 4)
            nc.scalar.activation(xT[:, 12:16, :].rearrange("p g d -> p (g d)"),
                                 ps[:, 7, :], ACT.Copy).then_inc(xt_done, 1)
            act.wait_ge(df_done, 1)
            nc.scalar.activation(flat(ex), flat(df), ACT.Exp).then_inc(ex_done, 1)
            act.wait_ge(half_set, 1)
            nc.scalar.activation(warm[:, 0:1], half[:, 0:1], ACT.Gelu)
            act.wait_ge(b1_in, 16)
            act.wait_ge(eidx_done, 1)

            def step(t, par):
                e = act.value_load(eidx[0:1, bass.ds(t, 1)], min_val=0, max_val=NE - 1)
                act.wait_ge(h_psum, t + 1)
                if not plain(t) or t >= 2:
                    act.wait_ge(y_psum, t - 1)
                for c in range(C):
                    last = nc.scalar.activation(hT[:, par, c, :], ps[:, 2 + par, c * P:(c + 1) * P], ACT.Gelu,
                                                bias=b1_sb[:, bass.ds(e, 1), c])
                last.then_inc(h_done, 1)

            tiles(act, step, 0, TILES - 1)

        @block.gpsimd
        def _(pool):
            nc.gpsimd.memset(ones_sb[:], 1.0).then_inc(ones_set, 1)
            nc.gpsimd.memset(half[:], -0.5).then_inc(half_set, 1)
            nc.gpsimd.memset(xs[:, :, 0:TOK], 0.0).then_inc(blank_set, 1)
            nc.gpsimd.memset(xs.bitcast(I32)[:, :, TOK:TOK + 1], B * N).then_inc(blank_set, 1)
            pool.wait_ge(half_set, 1)

            def inv_sqrt(n, g0, g1):
                pool.wait_ge(var_done, n)
                nc.gpsimd.tensor_tensor(rstd[:, g0:g1], var[:, g0:g1], half[:, g0:g1], ALU.pow).then_inc(rstd_done, 1)

            inv_sqrt(1, 0, G // 2)
            inv_sqrt(2, G // 2, G)
            for kt in range(KT):
                pool.wait_ge(t_copied, kt + 1)
                nc.gpsimd.tensor_scalar(k0i[:, kt, 0, :], ts[:, kt, 0, 1, :], -1.0, 1.0, ALU.mult, ALU.mult).then_inc(k0_done, 1)
                nc.gpsimd.tensor_copy(k0i[:, kt, 1, :], ts[:, kt, 0, 1, :]).then_inc(k0_done, 1)
            pool.wait_ge(tok_in, 16)
            nc.gpsimd.tensor_copy(rg.bitcast(I32)[:, :, TOK], tok_sb[:]).then_inc(tok_set, 1)
            pool.wait_ge(xn_done, G)
            inv_sqrt(3, 0, G // 2)
            inv_sqrt(4, G // 2, G)
            pool.wait_ge(tok_set, 1)
            pool.wait_ge(blank_out, 16)
            pool.wait_ge(row_done, 3)
            pool.wait_ge(slot_done, 1)
            for g in range(G):
                nc.gpsimd.indirect_dma_start(
                    out=scratch.ap(), out_offset=bass.IndirectOffsetOnAxis(ap=slot[:, g:g + 1], axis=0),
                    in_=rg[:, g, :], in_offset=None).then_inc(rows_out, 16)

            for t in range(TILES):
                pool.wait_ge(o_done, t + 1)
                nc.gpsimd.indirect_dma_start(
                    out=out, out_offset=bass.IndirectOffsetOnAxis(ap=ib[:, t % 2, :], axis=0),
                    in_=ob[:, t % 2, :], in_offset=None, bounds_check=B * N - 1, oob_is_err=False
                ).then_inc(o_out[t % 2], 16)
            pool.wait_ge(o_out[0], 16 * ((TILES + 1) // 2))
            pool.wait_ge(o_out[1], 16 * (TILES // 2))

        @block.vector
        def _(dve):
            done = [0]

            def link(ins):
                done[0] += 1
                ins.then_inc(dve_step, 1)
                dve.wait_ge(dve_step, done[0])

            def stats(src, g):
                nc.vector.bn_stats(st[:, g, :], src).then_inc(dve_step, 1)
                done[0] += 1

            def norm(n, g0, g1):
                dve.wait_ge(dve_step, done[0])
                for g in range(g0, g1):
                    last = nc.vector.bn_aggr(mv[:, g, :], st[:, g, :])
                link(last)
                nc.vector.tensor_scalar(var[:, g0:g1], mv[:, g0:g1, 1], EPS, None, ALU.add).then_inc(var_done, 1)
                dve.wait_ge(rstd_done, n)
                nc.vector.scalar_tensor_tensor(nmr[:, g0:g1], mv[:, g0:g1, 0], -1.0, rstd[:, g0:g1],
                                               ALU.mult, ALU.mult).then_inc(nmr_done, 1)

            for k in range(BLK):
                for h in range(2):
                    dve.wait_ge(x_in[k][h], 16)
                    for g in range(8 * k + 4 * h, 8 * k + 4 * h + 4):
                        stats(xg[:, g, :], g)
                norm(k + 1, 8 * k, 8 * k + 8)

            dve.wait_ge(misc_in, 16)
            for kt in range(KT):
                dve.wait_ge(t_copied, kt + 1)
                nc.vector.scalar_tensor_tensor(k1r[:, kt, :], ts[:, kt, 0, 1, :], nalt, ts[:, kt, 1, 0, :], ALU.mult, ALU.add)
                nc.vector.scalar_tensor_tensor(k1i[:, kt, 0, :], ts[:, kt, 0, 0, :], nalt, ts[:, kt, 1, 1, :],
                                               ALU.mult, ALU.subtract)
                link(nc.vector.scalar_tensor_tensor(k1i[:, kt, 1, :], ts[:, kt, 0, 0, :], alt, ts[:, kt, 1, 1, :],
                                                    ALU.mult, ALU.add))

            def times(dst, spec, re, im):
                nc.vector.tensor_tensor(pr[:, dst].rearrange("p r (b d) -> p (r b) d", d=D),
                                        spec.rearrange("p r (b d) -> p (r b) d", d=D),
                                        re.unsqueeze(1).to_broadcast([P, 2 * B, D]), ALU.mult)
                return nc.vector.tensor_tensor(pr[:, dst + 1].rearrange("p r (b d) -> p r b d", d=D),
                                               spec[:, ::-1, :].rearrange("p r (b d) -> p r b d", d=D),
                                               im.unsqueeze(2).to_broadcast([P, 2, B, D]), ALU.mult)

            for kt in range(KT):
                spec = [ps[:, 4 * kt + 2 * k:4 * kt + 2 * k + 2, :] for k in range(BLK)]
                k0r = ts[:, kt, 0, 0, :]
                dve.wait_ge(k0_done, 2 * kt + 2)
                dve.wait_ge(x_spec, BLK * 2 * kt + 2)
                link(times(0, spec[0], k0r, k0i[:, kt]))
                nc.vector.tensor_tensor(ya[:, kt, 0], pr[:, 0], pr[:, 1], ALU.add).then_inc(y_spec, 1)
                link(times(2, spec[0], k1r[:, kt], k1i[:, kt]))
                link(nc.vector.tensor_tensor(ya[:, kt, 1], pr[:, 2], pr[:, 3], ALU.add))
                dve.wait_ge(y_spec, 2 * kt + 1)
                dve.wait_ge(x_spec, BLK * 2 * kt + 4)
                link(times(0, spec[1], k0r, k0i[:, kt]))
                link(nc.vector.tensor_tensor(pr[:, 2], pr[:, 0], pr[:, 1], ALU.add))
                nc.vector.tensor_tensor(ya[:, kt, 1], ya[:, kt, 1], pr[:, 2], ALU.add).then_inc(y_spec, 1)
                dve.wait_ge(y_spec, 2 * kt + 2)

            dve.wait_ge(xn_done, G)
            for k in range(BLK):
                for s in range(S):
                    dve.wait_ge(y_conv, 2 * k + s + 1)
                    link(nc.vector.tensor_tensor(rows[:, k, :, s, 0:D], x_sb[:, k, :, s, :],
                                                 ps[:, 2 * k + s, :].rearrange("p (b d) -> p b d", d=D), ALU.add))
                for g in range(8 * k, 8 * k + 8):
                    stats(rg[:, g, 0:D], g)
                norm(BLK + k + 1, 8 * k, 8 * k + 8)
            dve.wait_ge(nmr_done, 2 * BLK)
            nc.vector.tensor_copy(rg[:, :, RSTD], rstd[:]).then_inc(row_done, 1)
            nc.vector.tensor_copy(rg[:, :, NMR], nmr[:]).then_inc(row_done, 1)

            dve.wait_ge(gate_in, 32)
            dve.wait_ge(logits, 1)
            link(nc.vector.tensor_tensor(lg[:], lg_ps.rearrange("p (e g) -> p e g", g=G),
                                         gb_sb[:].unsqueeze(2).to_broadcast([P, NE, G]), ALU.add))
            link(nc.vector.tensor_reduce(m16[:, 0], by_group(lg), AX_X, ALU.max))
            nc.vector.tensor_tensor(df[:], lg[:], all_e(m16[:, 0]), ALU.subtract).then_inc(df_done, 1)
            dve.wait_ge(df_done, 1)
            link(nc.vector.scalar_tensor_tensor(flat(sc), flat(df), 0.0, pick, ALU.is_ge, ALU.mult))
            link(nc.vector.tensor_reduce(m16[:, 1], by_group(sc), AX_X, ALU.max))
            nc.vector.tensor_tensor(oh[:], sc[:], all_e(m16[:, 1]), ALU.is_equal).then_inc(oh_done, 1)
            dve.wait_ge(ex_done, 1)
            link(nc.vector.tensor_reduce(m16[:, 2], by_group(ex), AX_X, ALU.add))
            nc.vector.reciprocal(rg[:, :, WGT], m16[:, 2]).then_inc(row_done, 1)
            dve.wait_ge(counted, 1)
            link(nc.vector.tensor_tensor_scan(flat(inc), carry, tot_ps, 0.0, ALU.mult, ALU.add))
            link(nc.vector.tensor_scalar(cnt[:, 0], inc[:, :, G - 1], float(P - 1), None, ALU.add))
            link(nc.vector.tensor_scalar(cnt[:, 1], cnt[:, 0], 7, None, ALU.logical_shift_right))
            link(nc.vector.tensor_tensor_scan(ends[:, 0], ones_sb[:, 0:NE], cnt[:, 1], 0.0, ALU.mult, ALU.add))
            link(nc.vector.tensor_tensor(cmp[0:1], ends[0:1, 0].unsqueeze(1).to_broadcast([1, TILES, NE]), iota, ALU.is_le))
            link(nc.vector.tensor_reduce(ecnt[0:1, :], cmp[0:1], AX_X, ALU.add))
            nc.vector.tensor_scalar(eidx[0:1, 0:TILES], ecnt[0:1, :], float(NE - 1), None, ALU.min).then_inc(eidx_done, 1)
            link(nc.vector.tensor_tensor(ends[:, 1], ends[:, 0], cnt[:, 1], ALU.subtract))
            link(nc.vector.tensor_tensor(flat(inc), flat(inc), tot_ps, ALU.subtract))
            link(nc.vector.tensor_tensor(flat(inc), flat(inc), rank_ps, ALU.add))
            link(nc.vector.scalar_tensor_tensor(pos3[:], ends[:, 1].unsqueeze(2).to_broadcast([P, NE, G]), float(P),
                                                inc[:], ALU.mult, ALU.add))
            link(nc.vector.tensor_tensor(pos3[:], pos3[:], oh[:], ALU.mult))
            link(nc.vector.tensor_reduce(m16[:, 3], by_group(pos3), AX_X, ALU.add))
            link(nc.vector.tensor_copy(posi[:, 0], m16[:, 3]))
            nc.vector.tensor_scalar(posi[:, 1], posi[:, 0], P - 1, None, ALU.bitwise_and)
            link(nc.vector.tensor_scalar(posi[:, 2], posi[:, 0], 7, None, ALU.logical_shift_right))
            nc.vector.scalar_tensor_tensor(slot[:], posi[:, 1], float(TILES), posi[:, 2],
                                           ALU.mult, ALU.add).then_inc(slot_done, 1)

            dve.wait_ge(eidx_done, 1)
            dve.wait_ge(w1_in, 16)
            dve.wait_ge(b2_in, 16)
            dve.wait_ge(blank_out, 16)

            def finish(t, par):
                e = dve.value_load(eidx[0:1, bass.ds(t, 1)], min_val=0, max_val=NE - 1)
                dve.wait_ge(y_psum, t + 1)
                nc.vector.tensor_tensor(yb[:, par, :].unsqueeze(1), ps[:, 4 + par, 0:D].unsqueeze(1), b2_sb[:, bass.ds(e, 1), :],
                                        ALU.add).then_inc(yb_done, 1)
                if not plain(t) or t >= 2:
                    dve.wait_ge(o_out[par], (t - par) * 8)
                nc.vector.tensor_copy(ib[:, par, :], xs.bitcast(U32)[:, bass.ds(t, 1), TOK])
                dve.wait_ge(yb_done, t + 1)
                nc.vector.scalar_tensor_tensor(ob[:, par, :].unsqueeze(1), yb[:, par, :].unsqueeze(1),
                                               xs[:, bass.ds(t, 1), WGT],
                                               xs[:, bass.ds(t, 1), 0:D], ALU.mult, ALU.add).then_inc(o_done, 1)

            def step(t, par):
                if not plain(t) or t >= 1:
                    finish(t - 1, 1 - par)
                if not plain(t) or t + 3 < TILES:
                    u = t + 3
                    if plain(t) and u == 0:
                        dve.wait_ge(xs_in[0], 16)
                    if plain(t) and u == FIRST - 1:
                        dve.wait_ge(xs_in[1], 16)
                    if not plain(t) or u >= 2:
                        dve.wait_ge(xsT_psum, u - 1)
                    nc.vector.tensor_scalar(xsn[:, 1 - par, :].unsqueeze(1), xs[:, bass.ds(u, 1), 0:D],
                                            xs[:, bass.ds(u, 1), RSTD], xs[:, bass.ds(u, 1), NMR],
                                            ALU.mult, ALU.add).then_inc(xsn_done, 1)
                if not plain(t) or 0 <= t + 2 < TILES:
                    u = t + 2
                    e = dve.value_load(eidx[0:1, bass.ds(u, 1)], min_val=0, max_val=NE - 1)
                    if not plain(t) or u >= 2:
                        dve.wait_ge(h_psum, u - 1)
                    nc.vector.tensor_copy(wst[:, par], w1_sb[:, bass.ds(e, 1), :].rearrange("p e (q c) -> p (e c) q", c=C)
                                          ).then_inc(wst_done, 1)
                    dve.wait_ge(xsT_psum, u + 1)
                    nc.vector.tensor_copy(xsT[:, par, :], ps[:, par, 0:P]).then_inc(xsT_done, 1)

            tiles(dve, step, -3, TILES)

        @block.tensor
        def _(pe):
            def transform(dst, kt, ri, rhs):
                for s in range(S):
                    last = nc.tensor.matmul(dst, fwd_sb[:, s, kt, ri, :], rhs[s], start=(s == 0), stop=(s == S - 1))
                return last

            pe.wait_ge(fwd_in, 16)
            pe.wait_ge(t_in, 16)
            for kt in range(KT):
                for k in range(BLK):
                    for ri in range(2):
                        q = (2 * k + ri) * D
                        last = transform(ps[:, 6 + kt, q:q + D], kt, ri, [t_sb[:, k, s, :] for s in range(S)])
                last.then_inc(t_spec, 1)
            for kt in range(KT):
                for k in range(BLK):
                    pe.wait_ge(xn_done, G // BLK * (k + 1))
                    for ri in range(2):
                        bank = 4 * kt + 2 * k + ri
                        if bank >= 6:
                            pe.wait_ge(t_copied, bank - 5)
                        transform(ps[:, bank, :], kt, ri, [xn[:, k, :, s, :] for s in range(S)]).then_inc(x_spec, 1)
            pe.wait_ge(inv_in, 16)
            for kt in range(KT):
                pe.wait_ge(y_spec, 2 * kt + 2 if kt == 0 else 2 * kt + 1)
                for k in range(BLK):
                    if kt and k:
                        pe.wait_ge(y_spec, 2 * kt + 2)
                    for s in range(S):
                        for ri in range(2):
                            last = nc.tensor.matmul(ps[:, 2 * k + s, :], inv_sb[:, kt, ri, s, :], ya[:, kt, k, ri, :],
                                                    start=(kt == 0 and ri == 0), stop=(kt == KT - 1 and ri == 1))
                        if kt == KT - 1:
                            last.then_inc(y_conv, 1)
            pe.wait_ge(misc_in, 16)
            pe.wait_ge(gate_in, 32)
            for q in range(G // 4):
                for g in range(4 * q, 4 * q + 4):
                    pe.wait_ge(xn_done, G + g + 1)
                    last = nc.tensor.transpose(ps[:, 4 + q, (g % 4) * P:(g % 4 + 1) * P], xng[:, g, :], ident)
                last.then_inc(xt_psum, 1)
            lg_v = lg_ps.rearrange("p (e g) -> p g e", g=G)
            for g in range(G):
                if g % 4 == 0:
                    pe.wait_ge(xt_done, g // 4 + 1)
                last = nc.tensor.matmul(lg_v[:, g, :], xT[:, g, :], gw_sb[:], start=True, stop=True)
            last.then_inc(logits, 1)
            pe.wait_ge(oh_done, 1)
            pe.wait_ge(ones_set, 1)
            nc.tensor.matmul(rank_ps, tri, flat(oh), start=True, stop=True)
            nc.tensor.matmul(tot_ps, ones_sb[:], flat(oh), start=True, stop=True).then_inc(counted, 1)

            pe.wait_ge(w2_in, 16)
            pe.wait_ge(eidx_done, 1)
            pe.wait_ge(slot_done, 1)

            def step(t, par):
                if not plain(t) or t + 2 < TILES:
                    u = t + 2
                    pe.wait_ge(xsn_done, u + 1)
                    if not plain(t) or u >= 2:
                        pe.wait_ge(xsT_done, u - 1)
                    nc.tensor.transpose(ps[:, par, 0:P], xsn[:, par, :], ident).then_inc(xsT_psum, 1)
                if not plain(t) or 0 <= t + 1 < TILES:
                    u = t + 1
                    pe.wait_ge(xsT_done, u + 1)
                    pe.wait_ge(wst_done, u + 1)
                    if not plain(t) or u >= 2:
                        pe.wait_ge(h_done, u - 1)
                    for c in range(C):
                        last = nc.tensor.matmul(ps[:, 3 - par, c * P:(c + 1) * P], wst[:, 1 - par, c, :],
                                                xsT[:, 1 - par, :], start=True, stop=True)
                    last.then_inc(h_psum, 1)
                if not plain(t) or t >= 0:
                    e = pe.value_load(eidx[0:1, bass.ds(t, 1)], min_val=0, max_val=NE - 1)
                    pe.wait_ge(h_done, t + 1)
                    if not plain(t) or t >= 2:
                        pe.wait_ge(yb_done, t - 1)
                    for c in range(C):
                        last = nc.tensor.matmul(ps[:, 4 + par, 0:D], hT[:, par, c, :], w2_sb[:, bass.ds(e, 1), c, :],
                                                start=(c == 0), stop=(c == C - 1))
                    last.then_inc(y_psum, 1)

            tiles(pe, step, -2, TILES - 1)


_INS = ['L0_attn_x', 'L0_attn_t', 'L0_ffn_gate_w', 'L0_ffn_gate_b', 'L0_ffn_w1', 'L0_ffn_b1', 'L0_ffn_w2', 'L0_ffn_b2']


def _constants(np):
    L = 2 * N // BLK
    k = np.arange(L // 2)
    n = np.arange(N // BLK)
    th = 2 * np.pi * np.outer(n, k + 0.5) / L
    f = np.stack([np.cos(th), -np.sin(th)], 1)
    fwd = f.reshape(P, S, 2, KT, P).transpose(0, 1, 3, 2, 4)
    inv = (f * (2.0 / L)).reshape(P, S, 2, KT, P).transpose(4, 3, 2, 1, 0)
    misc = np.zeros((P, M_COLS))
    misc[:, M_ID:M_ID + P] = np.eye(P)
    misc[:, M_TRI:M_TRI + P] = np.triu(np.ones((P, P)), 1)
    misc[:, M_ALT] = 1 - 2 * (np.arange(P) % 2)
    misc[:, M_ALT + 1] = -misc[:, M_ALT]
    misc[:, M_PICK:M_PICK + P] = np.repeat(np.arange(NE, 0, -1), G)
    misc[:, M_CARRY:M_CARRY + P] = np.tile(np.arange(G) > 0, NE)
    misc[:, M_IOTA:] = np.repeat(np.arange(TILES), NE)
    kk, bb, ss = np.meshgrid(np.arange(BLK), np.arange(B), np.arange(S), indexing="ij")
    tok = (bb * N + kk * (N // BLK) + ss).reshape(1, G) + S * np.arange(P)[:, None]
    return (fwd.reshape(P, -1).astype(np.float32), inv.reshape(P, -1).astype(np.float32),
            misc.astype(np.float32), tok.astype(np.int32))


def kernel(**inputs):
    import numpy as _np
    import concourse.bacc as _bacc
    from concourse import mybir as _mybir
    from concourse.bass_utils import run_bass_kernel_spmd as _run

    nc = _bacc.Bacc("TRN2", target_bir_lowering=False, num_devices=1)
    arrays, args = {}, []
    named = [(n, _np.ascontiguousarray(inputs[n])) for n in _INS]
    named += list(zip(("fwd", "inv", "misc", "tok"), map(_np.ascontiguousarray, _constants(_np))))
    for name, a in named:
        arrays[f"in_{name}_dram"] = a
        args.append(nc.dram_tensor(f"in_{name}_dram", a.shape, _mybir.dt.from_np(a.dtype), kind="ExternalInput").ap())
    out = nc.dram_tensor("out_0_dram", (B * N, D), _mybir.dt.float32, kind="ExternalOutput").ap()
    build(nc, *args, out)
    r = _run(nc, [arrays], core_ids=[0])
    return r.results[0]["out_0_dram"].reshape(B, N, D)
```

```python
from contextlib import ExitStack

import concourse.bass as bass
from concourse import mybir

P = 128
ALU = mybir.AluOpType
ACT = mybir.ActivationFunctionType
F32 = mybir.dt.float32
I32 = mybir.dt.int32
U32 = mybir.dt.uint32
AX_X = mybir.AxisListType.X

B, N, D = 4, 512, 128
BLK = 2
S = N // BLK // P
KT = N // 2 // P
G = BLK * B * S
NE = 8
FF = 512
C = FF // P
TILES = G + NE - 1
EPS = 1e-5
ROW = D + 4
RSTD, NMR, WGT, TOK = D, D + 1, D + 2, D + 3
REGION = B * N + P
BLANK = NE * REGION
HG = G // BLK
CH = BLK * S
NOB = 4


def full_tiles(chunks):
    return -(-(chunks * B * P - NE * (P - 1)) // P)


PHASES = ((3, full_tiles(3)), (CH, TILES - full_tiles(3)))
WARM = 11
ON_ACT = (2, 3, 4, 4)
ON_ACT2 = 2

CORE = G + NE // 2

M_ID, M_RANK, M_ALT, M_PICK, M_CARRY = 0, P, 2 * P, 2 * P + 2, 2 * P + 2 + NE * B
M_IOTA = M_CARRY + NE * (B + 1)
M_REG = M_IOTA + 1
M_SEED = M_REG + NE
M_FIRST = M_SEED + NE
M_COLS = M_FIRST + NE


def build(nc, x, taps, gate_w, gate_b, w1, b1, w2, b2, fwd, inv, misc, tok, out):
    with ExitStack() as ctx:
        def sb(name, shape, dt=F32):
            return ctx.enter_context(nc.sbuf_tensor(name, shape, dt))

        def sem(name):
            return ctx.enter_context(nc.semaphore(name))

        x_sb = sb("x_sb", [P, BLK, B, S, D])
        xn = sb("xn", [P, BLK, S, B, D])
        t_sb = sb("t_sb", [P, BLK, S, D])
        fwd_sb = sb("fwd_sb", [P, S, KT, 2, P])
        inv_sb = sb("inv_sb", [P, KT, 2, S, P])
        misc_sb = sb("misc_sb", [P, M_COLS])
        ones_sb = sb("ones_sb", [P, P])
        tok_sb = sb("tok_sb", [P, G], I32)
        gw_sb = sb("gw_sb", [P, NE])
        gb_sb = sb("gb_sb", [P, NE])
        w1_sb = sb("w1_sb", [P, NE, FF])
        w2_sb = sb("w2_sb", [P, NE, C, D])
        b1_sb = sb("b1_sb", [P, NE, C])
        b2_sb = sb("b2_sb", [P, NE, D])
        st = sb("st", [P, G, 6])
        mv = sb("mv", [P, G, 2])
        var = sb("var", [P, G])
        half = sb("half", [P, G])
        rstd = sb("rstd", [P, G])
        nmr = sb("nmr", [P, G])
        ts = sb("ts", [P, KT, BLK, 2, D])
        k0i = sb("k0i", [P, KT, 2, D])
        t_alt = sb("t_alt", [P, KT, 3, D])
        k1r = sb("k1r", [P, KT, D])
        k1i = sb("k1i", [P, KT, 2, D])
        pr = sb("pr", [P, KT, 3, 2, 2, N])
        ya = sb("ya", [P, KT, BLK, 2, N])
        rows = sb("rows", [P, G, ROW])
        xT = sb("xT", [P, G, P])
        df, ex, sc, pos = (sb(n, [P, CH, NE, B]) for n in ("df", "ex", "sc", "pos"))
        oh = sb("oh", [P, CH + 1, NE, 1 + B])
        cum = sb("cum", [P, CH, NE, 1 + B])
        m8 = sb("m8", [P, CH, 4, B])
        NP = len(PHASES)
        free = sb("free", [P, NP, NE])
        base = sb("base", [P, NP, NE])
        base_row = sb("base_row", [P, NP, NE])
        cnt = sb("cnt", [P, NP, NE])
        cnti = sb("cnti", [P, NP, 2, NE], I32)
        ends = sb("ends", [P, NP, 4, NE])
        freei = sb("freei", [P, NE], I32)
        slot = sb("slot", [P, G], U32)
        cmp = sb("cmp", [P, NP, 4, NE])
        ecnt = sb("ecnt", [P, NP, 2])
        eidx = sb("eidx", [P, NP], I32)
        usedi = sb("usedi", [P, 1], I32)
        tfirst = sb("tfirst", [P, NP], I32)
        blank = sb("blank", [P, ROW])
        xs = sb("xs", [P, TILES, ROW])
        xsn = sb("xsn", [P, 4, D])
        xsT = sb("xsT", [P, 4, P])
        wst = sb("wst", [P, 4, C, P])
        hT = sb("hT", [P, 2, C, P])
        yb = sb("yb", [P, 2, D])
        ob = sb("ob", [P, NOB, D])
        ib = sb("ib", [P, NOB, 1], U32)
        warm = sb("warm", [P, 2])
        ps = ctx.enter_context(nc.psum_tensor("ps", [P, 8, 512], F32))
        scratch = nc.dram_tensor("scratch", [BLANK + P, ROW], F32)

        x_in = [[sem(f"x_in{k}{h}") for h in range(2)] for k in range(BLK)]
        t_in, fwd_in, inv_in, misc_in, tok_in = (sem(n) for n in ("t_in", "fwd_in", "inv_in", "misc_in", "tok_in"))
        gate_in, w1_in, w2_in, b1_in, b2_in = (sem(n) for n in ("gate_in", "w1_in", "w2_in", "b1_in", "b2_in"))
        dve_step = sem("dve_step")
        pool_step = sem("pool_step")
        ones_set = sem("ones_set")
        half_set = sem("half_set")
        blank_set, blank_out = sem("blank_set"), sem("blank_out")
        free_row, bn_done, seeded = sem("free_row"), sem("bn_done"), sem("seeded")
        var_done, rstd_done, nmr_done = sem("var_done"), sem("rstd_done"), sem("nmr_done")
        xn_act, xn_dve = sem("xn_act"), sem("xn_dve")
        t_spec, t_copied, k0_done, alt_done, k1_done = (sem(n) for n in ("t_spec", "t_copied", "k0_done", "alt_done", "k1_done"))
        x_spec, prods, y_conv = sem("x_spec"), sem("prods"), sem("y_conv")
        y_spec = [sem(f"y_spec{kt}") for kt in range(KT)]
        sums = sem("sums")
        tok_set = sem("tok_set")
        xt_psum, xt_done, logits = sem("xt_psum"), sem("xt_done"), sem("logits")
        df_done, ex_done, oh_done, cum_done, ranked = (sem(n) for n in ("df_done", "ex_done", "oh_done", "cum_done", "ranked"))
        free_done, blanks_out, tfirst_done = sem("free_done"), sem("blanks_out"), sem("tfirst_done")
        eidx_done, slot_done = sem("eidx_done"), sem("slot_done")
        rows_out = [sem(f"rows_out{i}") for i in range(NP)]
        xs_in = [sem(f"xs_in{n}") for n in range(TILES)]
        xsn_done, xsT_psum, xsT_done = sem("xsn_done"), sem("xsT_psum"), sem("xsT_done")
        wst_done, h_psum, h_done = sem("wst_done"), sem("h_psum"), sem("h_done")
        y_psum, yb_done, o_done = sem("y_psum"), sem("yb_done"), sem("o_done")
        o_out = [sem(f"o_out{n}") for n in range(NOB)]

        xng = xn.rearrange("p k s b d -> p (k s b) d")
        ident = misc_sb[:, M_ID:M_ID + P]
        rank_w = misc_sb[:, M_RANK:M_RANK + P]
        alt, nalt = misc_sb[:, M_ALT:M_ALT + 1], misc_sb[:, M_ALT + 1:M_ALT + 2]
        pick = misc_sb[:, M_PICK:M_PICK + NE * B]
        carry = misc_sb[:, M_CARRY:M_IOTA]
        iota = misc_sb[:, M_IOTA:M_REG]
        tile_row = misc_sb[:, M_FIRST:M_COLS]
        region = misc_sb[:, M_REG:M_SEED]
        seed = misc_sb[:, M_SEED:M_FIRST]
        lg_ps = [ps[:, c, 0:NE * B] for c in range(CH)]
        rank_ps = [ps[:, c, NE * B:2 * NE * B] for c in range(CH)]
        free_ps = [ps[:, 6, i * NE:(i + 1) * NE] for i in range(NP)]

        def x_group(g):
            k, s, b = g // HG, g // B % S, g % B
            return x_sb[:, k, b, s, :]

        def load_groups(n):
            return [n // 2 * HG + s * B + n % 2 * 2 + b for s in range(S) for b in range(2)]

        def x_normalized(eng, n):
            eng.wait_ge(xn_act, sum(ON_ACT[:n]))
            eng.wait_ge(xn_dve, sum(4 - a for a in ON_ACT[:n]))

        def halves(a, k, h):
            return a.rearrange("p (k s h b) -> p k h s b", k=BLK, s=S, h=2)[:, k, h]

        def flat(a):
            return a.rearrange("p e g -> p (e g)")

        def by_group(a):
            return a.rearrange("p e g -> p g e")

        def all_e(a):
            return a.unsqueeze(1).to_broadcast([P, NE, B])


        def blank_tails(eng, experts):
            eng.wait_ge(free_done, 1)
            for e in experts:
                r = eng.value_load(freei[0:1, e:e + 1], min_val=0, max_val=BLANK - P)
                eng.dma_start(scratch[bass.ds(r, P), :], blank[:]).then_inc(blanks_out, 16)

        def phase_of(t):
            i = 0
            while t >= PHASES[i][1]:
                t -= PHASES[i][1]
                i += 1
            return i, t

        def load_tile(eng, t):
            i, n = phase_of(t)
            if n == 0:
                eng.wait_ge(tfirst_done, i + 1)
                eng.wait_ge(rows_out[i], 16 * B * (PHASES[i][0] - (PHASES[i - 1][0] if i else 0)))
                if i == NP - 1:
                    eng.wait_ge(blanks_out, 16 * (NE + 1))
            r = eng.value_load(tfirst[n:n + 1, i:i + 1], min_val=0, max_val=BLANK)
            eng.dma_start(xs[:, t, :], scratch[bass.ds(r, P), :]).then_inc(xs_in[t], 16)

        def all_tiles(eng, run):
            run(0, CORE)
            eng.wait_ge(eidx_done, NP)
            used = eng.value_load(usedi[0:1, 0:1], min_val=0, max_val=PHASES[-1][1])
            with eng.If(used > CORE - TILES + PHASES[-1][1]):
                run(CORE, TILES)

        def expert_of(eng, t):
            i, n = phase_of(t)
            if n == 0:
                eng.wait_ge(eidx_done, i + 1)
            return eng.value_load(eidx[n:n + 1, i:i + 1], min_val=0, max_val=NE - 1)

        block = ctx.enter_context(nc.Block())

        @block.sync
        def _(sp):
            xv = x.rearrange("b (k p s) d -> k p b (s d)", k=BLK, s=S)

            def load_x(k, h):
                sp.dma_start(x_sb[:, k, 2 * h:2 * h + 2].rearrange("p b s d -> p b (s d)"),
                             xv[k, :, 2 * h:2 * h + 2, :]).then_inc(x_in[k][h], 16)

            load_x(0, 0)
            sp.dma_start(fwd_sb.rearrange("p a b c d -> p (a b c d)"), fwd).then_inc(fwd_in, 16)
            load_x(0, 1)
            load_x(1, 0)
            load_x(1, 1)
            sp.dma_start(inv_sb.rearrange("p a b c d -> p (a b c d)"), inv).then_inc(inv_in, 16)
            sp.dma_start(tok_sb[:], tok).then_inc(tok_in, 16)
            sp.dma_start(gw_sb[:], gate_w).then_inc(gate_in, 16)
            sp.dma_start(gb_sb[0:1, :], gate_b.partition_broadcast(1)).then_inc(gate_in, 16)
            sp.dma_start(b1_sb[:], b1.rearrange("e (p c) -> p e c", c=C)).then_inc(b1_in, 16)
            sp.dma_start(b2_sb.rearrange("p e d -> p (e d)"),
                          b2.rearrange("e d -> (e d)").partition_broadcast(P)).then_inc(b2_in, 16)
            sp.dma_start(w1_sb[:], w1.rearrange("e d f -> d e f")).then_inc(w1_in, 16)
            sp.dma_start(w2_sb.rearrange("p e c d -> p e (c d)"),
                         w2.rearrange("e (p c) d -> p e (c d)", c=C)).then_inc(w2_in, 16)
            sp.wait_ge(blank_set, 2)
            sp.dma_start(scratch[BLANK:BLANK + P, :], blank[:]).then_inc(blanks_out, 16)
            blank_tails(sp, range(2))

            def load(first, last):
                for t in range(first, last):
                    load_tile(sp, t)

            all_tiles(sp, load)

        @block.scalar
        def _(act):
            act.dma_start(t_sb.rearrange("p k s d -> p k (s d)"),
                          taps.rearrange("(k p s) d -> p k (s d)", k=BLK, s=S)).then_inc(t_in, 16)
            act.dma_start(misc_sb[:], misc).then_inc(misc_in, 16)
            act.wait_ge(half_set, 1)
            nc.scalar.activation(warm[:, 1:2], half[:, 0:1], ACT.Identity)

            def normalize(src, g, scale, bias):
                nc.scalar.activation(xng[:, g, :], src, ACT.Identity, bias=bias, scale=scale).then_inc(xn_act, 1)

            for n in range(2 * BLK):
                act.wait_ge(nmr_done, n + 1)
                for g in load_groups(n)[:ON_ACT[n]]:
                    normalize(x_group(g), g, rstd[:, g:g + 1], nmr[:, g:g + 1])
                if n == 1:
                    for kt in range(KT):
                        act.wait_ge(t_spec, kt + 1)
                        nc.scalar.activation(ts[:, kt].rearrange("p k r d -> p (k r d)"), ps[:, 6 + kt, :],
                                             ACT.Copy).then_inc(t_copied, 1)
                    for kt in range(KT):
                        act.wait_ge(t_copied, kt + 1)
                        nc.scalar.activation(k0i[:, kt, 0, :], ts[:, kt, 0, 1, :], ACT.Copy, scale=-1.0).then_inc(k0_done, 1)
                        nc.scalar.activation(k0i[:, kt, 1, :], ts[:, kt, 0, 1, :], ACT.Copy).then_inc(k0_done, 1)
                    act.wait_ge(misc_in, 16)
                    for kt in range(KT):
                        nc.scalar.activation(t_alt[:, kt, 0:2, :], ts[:, kt, 0], ACT.Copy, scale=alt).then_inc(alt_done, 1)
                        nc.scalar.activation(t_alt[:, kt, 2, :], ts[:, kt, 0, 0, :], ACT.Copy, scale=nalt).then_inc(alt_done, 1)

            def gate_exp(c):
                act.wait_ge(df_done, c + 1)
                nc.scalar.activation(flat(ex[:, c]), flat(df[:, c]), ACT.Exp).then_inc(ex_done, 1)

            act.wait_ge(x_spec, 3 * BLK * KT)
            for c in range(CH):
                act.wait_ge(nmr_done, 2 * BLK + c + 1)
                for g in range(B * c, B * c + ON_ACT2):
                    normalize(rows[:, g, 0:D], g, rows[:, g, RSTD:RSTD + 1], rows[:, g, NMR:NMR + 1])
                if c >= 1:
                    gate_exp(c - 1)
                act.wait_ge(xt_psum, c + 1)
                nc.scalar.activation(xT[:, B * c:B * c + B, :].rearrange("p g d -> p (g d)"),
                                     ps[:, CH + c % 2, :], ACT.Copy).then_inc(xt_done, 1)
            gate_exp(CH - 1)
            act.wait_ge(half_set, 1)
            nc.scalar.activation(warm[:, 0:1], half[:, 0:1], ACT.Gelu)
            act.wait_ge(blank_set, 2)
            blank_tails(act, range(2, NE))
            act.wait_ge(b1_in, 16)

            def step(t, par):
                e = expert_of(act, t)
                act.wait_ge(h_psum, t + 1)
                if t >= 2:
                    act.wait_ge(y_psum, t - 1)
                for c in range(C):
                    nc.scalar.activation(hT[:, par % 2, c, :], ps[:, 2 + par % 2, c * P:(c + 1) * P], ACT.Gelu,
                                         bias=b1_sb[:, bass.ds(e, 1), c]).then_inc(h_done, 1)

            def activations(first, last):
                for t in range(first, last):
                    step(t, t % 4)

            all_tiles(act, activations)

        @block.gpsimd
        def _(pool):
            nc.gpsimd.memset(ones_sb[:], 1.0).then_inc(ones_set, 1)
            nc.gpsimd.memset(half[:], -0.5).then_inc(half_set, 1)
            nc.gpsimd.memset(blank[:, 0:TOK], 0.0).then_inc(blank_set, 1)
            nc.gpsimd.memset(blank.bitcast(I32)[:, TOK:TOK + 1], B * N).then_inc(blank_set, 1)
            pool.wait_ge(half_set, 1)

            def inv_sqrt(n, r, v, w, mr):
                pool.wait_ge(var_done, n + 1)
                nc.gpsimd.tensor_tensor(r, v, w, ALU.pow).then_inc(rstd_done, 1)
                pool.wait_ge(rstd_done, n + 1)
                nc.gpsimd.tensor_tensor(mr, mr, r, ALU.mult).then_inc(nmr_done, 1)

            for n in range(2 * BLK):
                inv_sqrt(n, *(halves(a, n // 2, n % 2) for a in (rstd, var, half, nmr)))
            for kt in range(KT):
                pool.wait_ge(alt_done, 2 * kt + 2)
                nc.gpsimd.tensor_tensor(k1r[:, kt, :], ts[:, kt, 1, 0, :], t_alt[:, kt, 1, :], ALU.subtract).then_inc(k1_done, 1)
                nc.gpsimd.tensor_tensor(k1i[:, kt, 0, :], t_alt[:, kt, 2, :], ts[:, kt, 1, 1, :], ALU.subtract).then_inc(k1_done, 1)
                nc.gpsimd.tensor_tensor(k1i[:, kt, 1, :], t_alt[:, kt, 0, :], ts[:, kt, 1, 1, :], ALU.add).then_inc(k1_done, 1)
            pool.wait_ge(tok_in, 16)
            nc.gpsimd.tensor_copy(rows.bitcast(I32)[:, :, TOK], tok_sb[:]).then_inc(tok_set, 1)
            for n, (kt, term) in enumerate(((0, 0), (1, 0), (0, 1), (1, 1))):
                pool.wait_ge(prods, n + 1)
                nc.gpsimd.tensor_tensor(ya[:, kt, term], pr[:, kt, term, 0], pr[:, kt, term, 1], ALU.add
                                        ).then_inc(sums if term else y_spec[kt], 1)
            pool.wait_ge(prods, 5)
            nc.gpsimd.tensor_tensor(pr[:, 0, 2, 0], pr[:, 0, 2, 0], pr[:, 0, 2, 1], ALU.add).then_inc(sums, 1)
            RSTD_AFTER = {2: 3}

            def scatter(g):
                phase = sum(g // B >= c for c, _ in PHASES)
                nc.gpsimd.indirect_dma_start(
                    out=scratch.ap(), out_offset=bass.IndirectOffsetOnAxis(ap=slot[:, g:g + 1], axis=0),
                    in_=rows[:, g, :], in_offset=None).then_inc(rows_out[phase], 16)

            pool.wait_ge(tok_set, 1)
            def inv_sqrt_x1(c):
                g0, g1 = B * c, B * c + B
                inv_sqrt(2 * BLK + c, rows[:, g0:g1, RSTD], var[:, g0:g1], half[:, g0:g1], rows[:, g0:g1, NMR])
            pool.wait_ge(sums, 3)
            nc.gpsimd.tensor_tensor(ya[:, 0, 1], ya[:, 0, 1], pr[:, 0, 2, 0], ALU.add).then_inc(y_spec[0], 1)
            inv_sqrt_x1(0)
            inv_sqrt_x1(1)
            inv_sqrt_x1(2)
            for g in range(G):
                if g % B == 0:
                    pool.wait_ge(slot_done, g // B + 1)
                if g in RSTD_AFTER:
                    inv_sqrt_x1(RSTD_AFTER[g])
                scatter(g)

            def results(first, last):
                for t in range(first, last):
                    pool.wait_ge(o_done, t + 1)
                    nc.gpsimd.indirect_dma_start(
                        out=out, out_offset=bass.IndirectOffsetOnAxis(ap=ib[:, t % NOB, :], axis=0),
                        in_=ob[:, t % NOB, :], in_offset=None, bounds_check=B * N - 1, oob_is_err=False
                    ).then_inc(o_out[t % NOB], 16)
                if last == TILES:
                    wait_results(last)

            def wait_results(tiles):
                for n in range(NOB):
                    pool.wait_ge(o_out[n], 16 * len(range(n, tiles, NOB)))

            all_tiles(pool, results)
            wait_results(CORE)

        @block.vector
        def _(dve):
            done = [0]

            def link(ins):
                done[0] += 1
                ins.then_inc(dve_step, 1)
                dve.wait_ge(dve_step, done[0])

            def bn(groups, src):
                for g in groups:
                    last = nc.vector.bn_stats(st[:, g, :], src(g))
                return last

            def aggregate(groups, pick, mr):
                for g in groups:
                    last = nc.vector.bn_aggr(mv[:, g, :], st[:, g, :])
                link(last)
                nc.vector.tensor_scalar(mr, pick(mv[:, :, 0]), -1.0, None, ALU.mult)
                nc.vector.tensor_scalar(pick(var), pick(mv[:, :, 1]), EPS, None, ALU.add).then_inc(var_done, 1)

            def normalize(g, src, r):
                nc.vector.tensor_scalar(xng[:, g, :], src, mv[:, g, 0:1], r, ALU.subtract, ALU.mult).then_inc(xn_dve, 1)

            def stats_x(n):
                dve.wait_ge(x_in[n // 2][n % 2], 16)
                link(bn(load_groups(n), x_group))
                def pick(a):
                    return halves(a, n // 2, n % 2)

                aggregate(load_groups(n), pick, pick(nmr))

            def normalize_x(n):
                dve.wait_ge(rstd_done, n + 1)
                for g in load_groups(n)[ON_ACT[n]:]:
                    normalize(g, x_group(g), rstd[:, g:g + 1])

            stats_x(0)
            normalize_x(0)
            stats_x(1)
            stats_x(2)
            normalize_x(1)
            stats_x(3)

            def times(kt, term, b0=0, b1=B):
                if term == 2:
                    spec = ps[:, 4 + 2 * kt:6 + 2 * kt, :]
                else:
                    spec = ps[:, b0 + kt, :].rearrange("p (r n) -> p r n", r=2)
                spec = spec.rearrange("p r (b d) -> p r b d", d=D)
                re = k1r[:, kt] if term == 1 else ts[:, kt, 0, 0, :]
                im = k1i[:, kt] if term == 1 else k0i[:, kt]
                to = pr[:, kt, term, :, :, b0 * D:b1 * D].rearrange("p n r (b d) -> p n r b d", d=D)
                nc.vector.tensor_tensor(to[:, 0], spec, re.unsqueeze(1).unsqueeze(1).to_broadcast([P, 2, b1 - b0, D]), ALU.mult)
                return nc.vector.tensor_tensor(to[:, 1], spec[:, ::-1], im.unsqueeze(2).to_broadcast([P, 2, b1 - b0, D]),
                                               ALU.mult)

            dve.wait_ge(k0_done, 2 * KT)
            for h in range(2):
                for kt in range(KT):
                    dve.wait_ge(x_spec, 4 * h + 2 * kt + 2)
                    last = times(kt, 0, 2 * h, 2 * h + 2)
                    if h:
                        last.then_inc(prods, 1)
            dve.wait_ge(k1_done, 3 * KT)
            for kt in range(KT):
                times(kt, 1, 0, 2)
                times(kt, 1, 2, 4).then_inc(prods, 1)
            for kt in range(KT):
                dve.wait_ge(x_spec, 10 + 2 * kt)
                times(kt, 2).then_inc(prods, 1)
            def last_spectrum():
                dve.wait_ge(prods, 6)
                link(nc.vector.tensor_tensor(pr[:, 1, 2, 0], pr[:, 1, 2, 0], pr[:, 1, 2, 1], ALU.add))
                dve.wait_ge(sums, 2)
                nc.vector.tensor_tensor(ya[:, 1, 1], ya[:, 1, 1], pr[:, 1, 2, 0], ALU.add).then_inc(y_spec[1], 1)

            def make_x1(c):
                k, s = c // S, c % S
                dve.wait_ge(y_conv, c + 1)
                link(nc.vector.tensor_tensor(rows[:, B * c:B * c + B, 0:D], x_sb[:, k, :, s, :],
                                             ps[:, c, :].rearrange("p (b d) -> p b d", d=D), ALU.add))
                bn(range(B * c, B * c + B), lambda g: rows[:, g, 0:D]).then_inc(bn_done, 1)

            def stats_x1(c):
                g0 = B * c
                dve.wait_ge(bn_done, c + 1)
                aggregate(range(g0, g0 + B), lambda a: a[:, g0:g0 + B], rows[:, g0:g0 + B, NMR])

            def normalize_x1(c):
                dve.wait_ge(rstd_done, 2 * BLK + c + 1)
                for g in range(B * c + ON_ACT2, B * c + B):
                    normalize(g, rows[:, g, 0:D], rows[:, g, RSTD:RSTD + 1])

            def choose(c):
                lg_v = lg_ps[c].rearrange("p (e g) -> p e g", g=B)
                dve.wait_ge(logits, c + 1)
                link(nc.vector.tensor_reduce(m8[:, c, 0], by_group(lg_v), AX_X, ALU.max))
                nc.vector.tensor_tensor(df[:, c], lg_v, all_e(m8[:, c, 0]), ALU.subtract).then_inc(df_done, 1)
                dve.wait_ge(df_done, c + 1)
                link(nc.vector.scalar_tensor_tensor(flat(sc[:, c]), flat(df[:, c]), 0.0, pick, ALU.is_ge, ALU.mult))
                link(nc.vector.tensor_reduce(m8[:, c, 1], by_group(sc[:, c]), AX_X, ALU.max))
                nc.vector.tensor_tensor(oh[:, c, :, 1:], sc[:, c], all_e(m8[:, c, 1]), ALU.is_equal).then_inc(oh_done, 1)
                dve.wait_ge(oh_done, c + 1)
                dve.wait_ge(seeded, c + 1)
                nc.vector.tensor_tensor_scan(flat(cum[:, c]), carry, flat(oh[:, c]), 0.0, ALU.mult, ALU.add).then_inc(cum_done, 1)
                dve.wait_ge(cum_done, c + 1)
                nc.vector.tensor_copy(oh[:, c + 1, :, 0], cum[:, c, :, B]).then_inc(seeded, 1)

            def weigh(c):
                dve.wait_ge(ex_done, c + 1)
                link(nc.vector.tensor_reduce(m8[:, c, 2], by_group(ex[:, c]), AX_X, ALU.add))
                nc.vector.reciprocal(rows[:, B * c:B * c + B, WGT], m8[:, c, 2])

            def place(c):
                dve.wait_ge(ranked, c + 1)
                link(nc.vector.tensor_tensor(pos[:, c], rank_ps[c].rearrange("p (e g) -> p e g", g=B), oh[:, c, :, 1:], ALU.mult))
                link(nc.vector.tensor_reduce(m8[:, c, 3], by_group(pos[:, c]), AX_X, ALU.add))
                nc.vector.tensor_copy(slot[:, B * c:B * c + B], m8[:, c, 3]).then_inc(slot_done, 1)

            nc.vector.tensor_copy(oh[:, 0, :, 0], seed).then_inc(seeded, 1)
            def count(i):
                dve.wait_ge(free_row, i + 1)
                link(nc.vector.tensor_copy(free[:, i], free_ps[i]))
                if i == NP - 1:
                    nc.vector.tensor_copy(freei[0:1, :], free[0:1, i]).then_inc(free_done, 1)

            def plan(i):
                b, br = (base[:, i], base_row[:, i]) if i else (region, tile_row)
                last, n = i == NP - 1, PHASES[i][1]
                end, start, m, taken = (ends[:, i, j] for j in range(4))
                link(nc.vector.tensor_tensor(cnt[:, i], free[:, i], b, ALU.subtract))
                link(nc.vector.tensor_scalar(cnti[:, i, 0], cnt[:, i], float(P - 1 if last else 0), None, ALU.add))
                link(nc.vector.tensor_scalar(cnti[:, i, 1], cnti[:, i, 0], 7, None, ALU.logical_shift_right))
                link(nc.vector.tensor_tensor_scan(end, ones_sb[:, 0:NE], cnti[:, i, 1], 0.0, ALU.mult, ALU.add))
                nc.vector.tensor_scalar(cmp[:, i, 0], end, iota, None, ALU.is_le)
                link(nc.vector.tensor_tensor(start, end, cnti[:, i, 1], ALU.subtract))
                nc.vector.tensor_reduce(ecnt[:, i, 0:1], cmp[:, i, 0], AX_X, ALU.add)
                nc.vector.scalar_tensor_tensor(cmp[:, i, 1], start, iota, cmp[:, i, 0], ALU.is_le, ALU.subtract)
                link(nc.vector.scalar_tensor_tensor(cmp[:, i, 2], start, float(-P), br, ALU.mult, ALU.add))
                if last:
                    nc.vector.tensor_copy(usedi[0:1, :], end[0:1, NE - 1:NE])
                nc.vector.tensor_scalar(eidx[:, i:i + 1], ecnt[:, i, 0:1], float(NE - 1), None, ALU.min).then_inc(eidx_done, 1)
                link(nc.vector.tensor_tensor(cmp[:, i, 3], cmp[:, i, 2], cmp[:, i, 1], ALU.mult))
                link(nc.vector.tensor_reduce(ecnt[:, i, 1:2], cmp[:, i, 3], AX_X, ALU.add))
                nc.vector.tensor_scalar(tfirst[:, i:i + 1], ecnt[:, i, 1:2], float(BLANK), None, ALU.add).then_inc(tfirst_done, 1)
                if not last:
                    link(nc.vector.tensor_scalar(m, start, float(n), None, ALU.min))
                    link(nc.vector.scalar_tensor_tensor(taken, end, float(n), m, ALU.min, ALU.subtract))
                    nc.vector.scalar_tensor_tensor(base[:, i + 1], taken, float(P), b, ALU.mult, ALU.add)
                    link(nc.vector.scalar_tensor_tensor(base_row[:, i + 1], taken, float(P), br, ALU.mult, ALU.add))

            last_spectrum()
            make_x1(0)
            stats_x1(0)
            make_x1(1)
            normalize_x1(0)
            stats_x1(1)
            make_x1(2)
            normalize_x1(1)
            stats_x1(2)
            choose(0)
            normalize_x1(2)
            weigh(0)
            place(0)
            make_x1(3)
            stats_x1(3)
            choose(1)
            normalize_x1(3)
            weigh(1)
            place(1)
            choose(2)
            weigh(2)
            place(2)
            count(0)
            plan(0)
            choose(3)
            weigh(3)
            place(3)
            count(1)
            plan(1)
            dve.wait_ge(w1_in, 16)
            dve.wait_ge(b2_in, 16)

            expert = {}

            def finish(t, par):
                e = expert.pop(t)
                w = xs[:, t, WGT:WGT + 1]
                nc.vector.scalar_tensor_tensor(yb[:, par % 2, :].unsqueeze(1), b2_sb[:, bass.ds(e, 1), :], w,
                                               xs[:, t, 0:D].unsqueeze(1), ALU.mult, ALU.add).then_inc(yb_done, 1)
                if t >= NOB:
                    dve.wait_ge(o_out[par], (t - par) * (16 // NOB))
                nc.vector.tensor_copy(ib[:, par, :], xs.bitcast(U32)[:, t, TOK:TOK + 1])
                dve.wait_ge(yb_done, t + 1)
                dve.wait_ge(y_psum, t + 1)
                nc.vector.scalar_tensor_tensor(ob[:, par, :], ps[:, 4 + par % 2, 0:D], w, yb[:, par % 2, :],
                                               ALU.mult, ALU.add).then_inc(o_done, 1)

            def hold_w1(u):
                e = expert[u] = expert_of(dve, u)
                if u >= 4:
                    dve.wait_ge(h_psum, u - 3)
                nc.vector.tensor_copy(wst[:, u % 4], w1_sb[:, bass.ds(e, 1), :].rearrange("p e (q c) -> p (e c) q", c=C)
                                      ).then_inc(wst_done, 1)

            def normalize_rows(u):
                dve.wait_ge(xs_in[u], 16)
                if u >= 4:
                    dve.wait_ge(xsT_psum, u - 3)
                nc.vector.tensor_scalar(xsn[:, u % 4, :], xs[:, u, 0:D], xs[:, u, RSTD:RSTD + 1], xs[:, u, NMR:NMR + 1],
                                        ALU.mult, ALU.add).then_inc(xsn_done, 1)

            def transposed(u):
                dve.wait_ge(xsT_psum, u + 1)
                if u >= 4:
                    dve.wait_ge(h_psum, u - 3)
                nc.vector.tensor_copy(xsT[:, u % 4, :], ps[:, u % 2, 0:P]).then_inc(xsT_done, 1)

            def tiles(first, last):
                for u in range(first, first + 3):
                    hold_w1(u)
                normalize_rows(first)
                for t in range(first - 2, last + 1):
                    if first <= t < last - 3:
                        hold_w1(t + 3)
                    if t == first - 2:
                        transposed(first)
                        normalize_rows(first + 1)
                    else:
                        if t + 3 < last:
                            normalize_rows(t + 3)
                        if t + 2 < last:
                            transposed(t + 2)
                    if t > first:
                        finish(t - 1, (t - 1) % 4)

            all_tiles(dve, tiles)

        @block.tensor
        def _(pe):
            def transform(dst, kt, ri, rhs):
                for s in range(S):
                    last = nc.tensor.matmul(dst, fwd_sb[:, s, kt, ri, :], rhs[s], start=(s == 0), stop=(s == S - 1))
                return last

            pe.wait_ge(ones_set, 1)
            for _ in range(WARM):
                nc.tensor.matmul(ps[:, 0, 0:P], ones_sb[:], ones_sb[:], start=True, stop=True)
            pe.wait_ge(fwd_in, 16)
            pe.wait_ge(t_in, 16)
            for kt in range(KT):
                for k in range(BLK):
                    for ri in range(2):
                        q = (2 * k + ri) * D
                        last = transform(ps[:, 6 + kt, q:q + D], kt, ri, [t_sb[:, k, s, :] for s in range(S)])
                last.then_inc(t_spec, 1)
            for k, b0, b1 in ((0, 0, 2), (0, 2, 4), (1, 0, 4)):
                x_normalized(pe, 2 * k + b1 // 2)
                for kt in range(KT):
                    for ri in range(2):
                        if k:
                            to = ps[:, 4 + 2 * kt + ri, :]
                        else:
                            to = ps[:, b0 + kt, ri * 2 * D:(ri + 1) * 2 * D]
                        if k and kt:
                            pe.wait_ge(t_copied, ri + 1)
                        transform(to, kt, ri, [xn[:, k, s, b0:b1, :] for s in range(S)]
                                  ).then_inc(x_spec, 1)
            def inverse(c, n):
                k, s = c // S, c % S
                kt = 1 - n if k else n
                pe.wait_ge(y_spec[kt], k + 1)
                for ri in range(2):
                    last = nc.tensor.matmul(ps[:, c, :], inv_sb[:, kt, ri, s, :], ya[:, kt, k, ri, :],
                                            start=(n == 0 and ri == 0), stop=(n == 1 and ri == 1))
                if n == 1:
                    last.then_inc(y_conv, 1)

            pe.wait_ge(inv_in, 16)
            pe.wait_ge(prods, 4)
            def transposes(c):
                pe.wait_ge(xn_act, sum(ON_ACT) + ON_ACT2 * (c + 1))
                pe.wait_ge(xn_dve, G - sum(ON_ACT) + (B - ON_ACT2) * (c + 1))
                if c >= 2:
                    pe.wait_ge(xt_done, c - 1)
                for b in range(B):
                    last = nc.tensor.transpose(ps[:, CH + c % 2, b * P:(b + 1) * P], xng[:, B * c + b, :], ident)
                last.then_inc(xt_psum, 1)

            def gate_logits(c):
                lg_v = lg_ps[c].rearrange("p (e g) -> p g e", g=B)
                nc.tensor.matmul(lg_v, ones_sb[0:1, :], gb_sb[0:1, :].unsqueeze(1).to_broadcast([1, B, NE]),
                                 start=True, stop=False)
                pe.wait_ge(xt_done, c + 1)
                for b in range(B):
                    last = nc.tensor.matmul(lg_v[:, b, :], xT[:, B * c + b, :], gw_sb[:], start=False, stop=(b == B - 1))
                last.then_inc(logits, 1)

            def keep_warm(n):
                for _ in range(n):
                    nc.tensor.matmul(ps[:, 7, 0:P], ones_sb[:], ones_sb[:], start=True, stop=True)

            def ranks(c):
                rank_v = rank_ps[c].rearrange("p (e g) -> p e g", g=B)
                pe.wait_ge(oh_done, c + 1)
                nc.tensor.matmul(rank_v, rank_w, oh[:, c, :, 1:], start=True, stop=False)
                pe.wait_ge(cum_done, c + 1)
                nc.tensor.matmul(rank_v, ones_sb[:], cum[:, c, :, 1:], start=False, stop=True).then_inc(ranked, 1)
                for i, (chunks, _) in enumerate(PHASES):
                    if chunks == c + 1:
                        nc.tensor.matmul(free_ps[i], ones_sb[:], cum[:, c, :, B], start=True, stop=True).then_inc(free_row, 1)

            inverse(0, 0)
            inverse(0, 1)
            inverse(1, 0)
            inverse(1, 1)
            inverse(2, 0)
            inverse(2, 1)
            pe.wait_ge(misc_in, 16)
            pe.wait_ge(gate_in, 32)
            pe.wait_ge(prods, 6)
            transposes(0)
            inverse(3, 0)
            gate_logits(0)
            inverse(3, 1)
            transposes(1)
            ranks(0)
            gate_logits(1)
            transposes(2)
            keep_warm(9)
            ranks(1)
            gate_logits(2)
            transposes(3)
            keep_warm(6)
            ranks(2)
            gate_logits(3)
            keep_warm(14)
            ranks(3)

            pe.wait_ge(w2_in, 16)
            pe.wait_ge(free_done, 1)
            keep_warm(22)

            def transpose_rows(u, par):
                if True:
                    pe.wait_ge(xsn_done, u + 1)
                    if u >= 2:
                        pe.wait_ge(xsT_done, u - 1)
                    nc.tensor.transpose(ps[:, par % 2, 0:P], xsn[:, (par + 2) % 4, :], ident).then_inc(xsT_psum, 1)

            def hidden(u, par):
                if True:
                    pe.wait_ge(xsT_done, u + 1)
                    pe.wait_ge(wst_done, u + 1)
                    if u >= 2:
                        pe.wait_ge(h_done, C * (u - 1))
                    for c in range(C):
                        last = nc.tensor.matmul(ps[:, 3 - par % 2, c * P:(c + 1) * P], wst[:, (par + 1) % 4, c, :],
                                                xsT[:, (par + 1) % 4, :], start=True, stop=True)
                    last.then_inc(h_psum, 1)

            def second(t, par):
                if True:
                    e = expert_of(pe, t)
                    if t >= 2:
                        pe.wait_ge(o_done, t - 1)
                    for c in range(C):
                        pe.wait_ge(h_done, C * t + c + 1)
                        last = nc.tensor.matmul(ps[:, 4 + par % 2, 0:D], hT[:, par % 2, c, :], w2_sb[:, bass.ds(e, 1), c, :],
                                                start=(c == 0), stop=(c == C - 1))
                    last.then_inc(y_psum, 1)

            def tiles(first, last):
                for t in range(first - 2, last):
                    par = t % 4
                    if t == first - 1:
                        hidden(first, par)
                        transpose_rows(first + 1, par)
                    else:
                        if t + 2 < last:
                            transpose_rows(t + 2, par)
                        if t + 1 < last and t >= first:
                            hidden(t + 1, par)
                    if t >= first:
                        second(t, par)

            all_tiles(pe, tiles)


_INS = ['L0_attn_x', 'L0_attn_t', 'L0_ffn_gate_w', 'L0_ffn_gate_b', 'L0_ffn_w1', 'L0_ffn_b1', 'L0_ffn_w2', 'L0_ffn_b2']


def _constants(np):
    L = 2 * N // BLK
    k = np.arange(L // 2)
    n = np.arange(N // BLK)
    th = 2 * np.pi * np.outer(n, k + 0.5) / L
    f = np.stack([np.cos(th), -np.sin(th)], 1)
    fwd = f.reshape(P, S, 2, KT, P).transpose(0, 1, 3, 2, 4)
    inv = (f * (2.0 / L)).reshape(P, S, 2, KT, P).transpose(4, 3, 2, 1, 0)
    misc = np.zeros((P, M_COLS))
    misc[:, M_ID:M_ID + P] = np.eye(P)
    misc[:, M_RANK:M_RANK + P] = np.triu(np.ones((P, P)), 1) - 1
    misc[:, M_ALT] = 1 - 2 * (np.arange(P) % 2)
    misc[:, M_ALT + 1] = -misc[:, M_ALT]
    misc[:, M_PICK:M_CARRY] = np.repeat(np.arange(NE, 0, -1), B)
    misc[:, M_CARRY:M_IOTA] = np.tile(np.arange(B + 1) > 0, NE)
    misc[:, M_IOTA] = np.arange(P)
    misc[:, M_REG:M_SEED] = np.arange(NE) * REGION
    misc[:, M_SEED:M_FIRST] = np.arange(NE) * (REGION // P)
    misc[:, M_FIRST:] = np.arange(NE) * REGION - BLANK + P * np.arange(P)[:, None]
    kk, ss, bb = np.meshgrid(np.arange(BLK), np.arange(S), np.arange(B), indexing="ij")
    tok = (bb * N + kk * (N // BLK) + ss).reshape(1, G) + S * np.arange(P)[:, None]
    return (fwd.reshape(P, -1).astype(np.float32), inv.reshape(P, -1).astype(np.float32),
            misc.astype(np.float32), tok.astype(np.int32))


def kernel(**inputs):
    import numpy as _np
    import concourse.bacc as _bacc
    from concourse import mybir as _mybir
    from concourse.bass_utils import run_bass_kernel_spmd as _run

    nc = _bacc.Bacc("TRN2", target_bir_lowering=False, num_devices=1)
    arrays, args = {}, []
    named = [(n, _np.ascontiguousarray(inputs[n])) for n in _INS]
    named += list(zip(("fwd", "inv", "misc", "tok"), map(_np.ascontiguousarray, _constants(_np))))
    for name, a in named:
        arrays[f"in_{name}_dram"] = a
        args.append(nc.dram_tensor(f"in_{name}_dram", a.shape, _mybir.dt.from_np(a.dtype), kind="ExternalInput").ap())
    out = nc.dram_tensor("out_0_dram", (B * N, D), _mybir.dt.float32, kind="ExternalOutput").ap()
    build(nc, *args, out)
    r = _run(nc, [arrays], core_ids=[0])
    return r.results[0]["out_0_dram"].reshape(B, N, D)
```

```python
from contextlib import ExitStack

import concourse.bass as bass
from concourse import mybir

P = 128
ALU = mybir.AluOpType
ACT = mybir.ActivationFunctionType
F32 = mybir.dt.float32
I32 = mybir.dt.int32
U32 = mybir.dt.uint32
AX_X = mybir.AxisListType.X

B, N, D = 4, 512, 128
BLK = 2
S = N // BLK // P
KT = N // 2 // P
G = BLK * B * S
NE = 8
FF = 512
C = FF // P
TILES = G + NE - 1
EPS = 1e-5
ROW = D + 4
RSTD, NMR, WGT, TOK = D, D + 1, D + 2, D + 3
REGION = B * N + P
BLANK = NE * REGION
HG = G // BLK
CH = BLK * S
NOB = 4


def full_tiles(chunks):
    return -(-(chunks * B * P - NE * (P - 1)) // P)


PHASES = ((3, full_tiles(3)), (CH, TILES - full_tiles(3)))
WARM = 9
ON_ACT = (2, 3, 4, 4)
ON_ACT2 = 2

CORE = G + NE // 2

M_ID, M_RANK, M_ALT, M_PICK, M_CARRY = 0, P, 2 * P, 2 * P + 2, 2 * P + 2 + NE * B
M_IOTA = M_CARRY + NE * (B + 1)
M_REG = M_IOTA + 1
M_SEED = M_REG + NE
M_FIRST = M_SEED + NE
M_COLS = M_FIRST + NE


def build(nc, x, taps, gate_w, gate_b, w1, b1, w2, b2, fwd, inv, misc, tok, out):
    with ExitStack() as ctx:
        def sb(name, shape, dt=F32):
            return ctx.enter_context(nc.sbuf_tensor(name, shape, dt))

        def sem(name):
            return ctx.enter_context(nc.semaphore(name))

        x_sb = sb("x_sb", [P, BLK, B, S, D])
        xn = sb("xn", [P, BLK, S, B, D])
        t_sb = sb("t_sb", [P, BLK, S, D])
        fwd_sb = sb("fwd_sb", [P, KT, S, 2, P])
        inv_sb = sb("inv_sb", [P, KT, 2, S, P])
        misc_sb = sb("misc_sb", [P, M_COLS])
        ones_sb = sb("ones_sb", [P, P])
        tok_sb = sb("tok_sb", [P, G], I32)
        gw_sb = sb("gw_sb", [P, NE])
        gb_sb = sb("gb_sb", [P, NE])
        w1_sb = sb("w1_sb", [P, NE, FF])
        w2_sb = sb("w2_sb", [P, NE, C, D])
        b1_sb = sb("b1_sb", [P, NE, C])
        b2_sb = sb("b2_sb", [P, NE, D])
        st = sb("st", [P, G, 6])
        mv = sb("mv", [P, G, 2])
        var = sb("var", [P, G])
        half = sb("half", [P, G])
        rstd = sb("rstd", [P, G])
        nmr = sb("nmr", [P, G])
        ts = sb("ts", [P, KT, BLK, 2, D])
        k0i = sb("k0i", [P, KT, 2, D])
        t_alt = sb("t_alt", [P, KT, 3, D])
        k1r = sb("k1r", [P, KT, D])
        k1i = sb("k1i", [P, KT, 2, D])
        pr = sb("pr", [P, KT, 3, 2, 2, N])
        ya = sb("ya", [P, KT, BLK, 2, N])
        rows = sb("rows", [P, G, ROW])
        xT = sb("xT", [P, G, P])
        df, ex, sc, pos = (sb(n, [P, CH, NE, B]) for n in ("df", "ex", "sc", "pos"))
        oh = sb("oh", [P, CH + 1, NE, 1 + B])
        cum = sb("cum", [P, CH, NE, 1 + B])
        red = sb("red", [P, CH, 4, B])
        NP = len(PHASES)
        free = sb("free", [P, NP, NE])
        base = sb("base", [P, NP, NE])
        base_row = sb("base_row", [P, NP, NE])
        cnt = sb("cnt", [P, NP, NE])
        cnti = sb("cnti", [P, NP, 2, NE], I32)
        ends = sb("ends", [P, NP, 4, NE])
        freei = sb("freei", [P, NE], I32)
        slot = sb("slot", [P, G], U32)
        cmp = sb("cmp", [P, NP, 4, NE])
        ecnt = sb("ecnt", [P, NP, 2])
        eidx = sb("eidx", [P, NP], I32)
        usedi = sb("usedi", [P, 1], I32)
        tfirst = sb("tfirst", [P, NP], I32)
        blank = sb("blank", [P, ROW])
        xs = sb("xs", [P, TILES, ROW])
        xsn = sb("xsn", [P, 4, D])
        xsT = sb("xsT", [P, 4, P])
        wst = sb("wst", [P, 4, C, P])
        hT = sb("hT", [P, 2, C, P])
        yb = sb("yb", [P, 2, D])
        ob = sb("ob", [P, NOB, D])
        ib = sb("ib", [P, NOB, 1], U32)
        warm = sb("warm", [P, 2])
        ps = ctx.enter_context(nc.psum_tensor("ps", [P, 8, 512], F32))
        scratch = nc.dram_tensor("scratch", [BLANK + P, ROW], F32)

        x_in = [[sem(f"x_in{k}{h}") for h in range(2)] for k in range(BLK)]
        t_in, inv_in, misc_in, tok_in = (sem(n) for n in ("t_in", "inv_in", "misc_in", "tok_in"))
        fwd_in = [sem(f"fwd_in{kt}") for kt in range(KT)]
        gate_in, w1_in, w2_in, b1_in, b2_in = (sem(n) for n in ("gate_in", "w1_in", "w2_in", "b1_in", "b2_in"))
        dve_step = sem("dve_step")
        ones_set = sem("ones_set")
        half_set = sem("half_set")
        blank_set = sem("blank_set")
        free_row, bn_done, seeded = sem("free_row"), sem("bn_done"), sem("seeded")
        var_done, rstd_done, nmr_done = sem("var_done"), sem("rstd_done"), sem("nmr_done")
        xn_act, xn_dve = sem("xn_act"), sem("xn_dve")
        t_spec, t_copied, k0_done, alt_done, k1_done = (sem(n) for n in ("t_spec", "t_copied", "k0_done", "alt_done", "k1_done"))
        x_spec, prods, y_conv = sem("x_spec"), sem("prods"), sem("y_conv")
        y_spec = [sem(f"y_spec{kt}") for kt in range(KT)]
        sums = sem("sums")
        tok_set = sem("tok_set")
        xt_psum, xt_done, logits = sem("xt_psum"), sem("xt_done"), sem("logits")
        df_done, ex_done, oh_done, cum_done, ranked = (sem(n) for n in ("df_done", "ex_done", "oh_done", "cum_done", "ranked"))
        free_done, blanks_out, tfirst_done = sem("free_done"), sem("blanks_out"), sem("tfirst_done")
        eidx_done, slot_done = sem("eidx_done"), sem("slot_done")
        rows_out = [sem(f"rows_out{i}") for i in range(NP)]
        xs_in = [sem(f"xs_in{n}") for n in range(TILES)]
        xsn_done, xsT_psum, xsT_done = sem("xsn_done"), sem("xsT_psum"), sem("xsT_done")
        wst_done, h_psum, h_done = sem("wst_done"), sem("h_psum"), sem("h_done")
        y_psum, yb_done, o_done = sem("y_psum"), sem("yb_done"), sem("o_done")
        o_out = [sem(f"o_out{n}") for n in range(NOB)]

        xng = xn.rearrange("p k s b d -> p (k s b) d")
        ident = misc_sb[:, M_ID:M_ID + P]
        rank_w = misc_sb[:, M_RANK:M_RANK + P]
        alt, nalt = misc_sb[:, M_ALT:M_ALT + 1], misc_sb[:, M_ALT + 1:M_ALT + 2]
        pick = misc_sb[:, M_PICK:M_PICK + NE * B]
        carry = misc_sb[:, M_CARRY:M_IOTA]
        iota = misc_sb[:, M_IOTA:M_REG]
        tile_row = misc_sb[:, M_FIRST:M_COLS]
        region = misc_sb[:, M_REG:M_SEED]
        seed = misc_sb[:, M_SEED:M_FIRST]
        lg_ps = [ps[:, c, 0:NE * B] for c in range(CH)]
        rank_ps = [ps[:, c, NE * B:2 * NE * B] for c in range(CH)]
        free_ps = [ps[:, 6, i * NE:(i + 1) * NE] for i in range(NP)]

        def x_group(g):
            k, s, b = g // HG, g // B % S, g % B
            return x_sb[:, k, b, s, :]

        def load_groups(n):
            return [n // 2 * HG + s * B + n % 2 * 2 + b for s in range(S) for b in range(2)]

        def x_normalized(eng, n):
            eng.wait_ge(xn_act, sum(ON_ACT[:n]))
            eng.wait_ge(xn_dve, sum(4 - a for a in ON_ACT[:n]))

        def halves(a, k, h):
            return a.rearrange("p (k s h b) -> p k h s b", k=BLK, s=S, h=2)[:, k, h]

        def flat(a):
            return a.rearrange("p e g -> p (e g)")

        def by_group(a):
            return a.rearrange("p e g -> p g e")

        def all_e(a):
            return a.unsqueeze(1).to_broadcast([P, NE, B])


        def blank_tails(eng, experts):
            eng.wait_ge(free_done, 1)
            for e in experts:
                r = eng.value_load(freei[0:1, e:e + 1], min_val=0, max_val=BLANK - P)
                eng.dma_start(scratch[bass.ds(r, P), :], blank[:]).then_inc(blanks_out, 16)

        def phase_of(t):
            i = 0
            while t >= PHASES[i][1]:
                t -= PHASES[i][1]
                i += 1
            return i, t

        def load_tile(eng, t):
            i, n = phase_of(t)
            if n == 0:
                eng.wait_ge(tfirst_done, i + 1)
                eng.wait_ge(rows_out[i], 16 * B * (PHASES[i][0] - (PHASES[i - 1][0] if i else 0)))
                if i == NP - 1:
                    eng.wait_ge(blanks_out, 16 * (NE + 1))
            r = eng.value_load(tfirst[n:n + 1, i:i + 1], min_val=0, max_val=BLANK)
            eng.dma_start(xs[:, t, :], scratch[bass.ds(r, P), :]).then_inc(xs_in[t], 16)

        def all_tiles(eng, step, ahead, behind=0):
            for t in range(-ahead, CORE - ahead):
                if t == CORE - ahead - 1:
                    eng.wait_ge(eidx_done, NP)
                    used = eng.value_load(usedi[0:1, 0:1], min_val=0, max_val=PHASES[-1][1])
                step(t, CORE)
            with eng.If(used > CORE - TILES + PHASES[-1][1]):
                for t in range(CORE - ahead, TILES + behind):
                    step(t, TILES)
            with eng.Else():
                for t in range(CORE - ahead, CORE + behind):
                    step(t, CORE)

        def expert_of(eng, t):
            i, n = phase_of(t)
            if n == 0:
                eng.wait_ge(eidx_done, i + 1)
            return eng.value_load(eidx[n:n + 1, i:i + 1], min_val=0, max_val=NE - 1)

        block = ctx.enter_context(nc.Block())

        @block.sync
        def _(sp):
            xv = x.rearrange("b (k p s) d -> k p b (s d)", k=BLK, s=S)

            def load_x(k, h):
                sp.dma_start(x_sb[:, k, 2 * h:2 * h + 2].rearrange("p b s d -> p b (s d)"),
                             xv[k, :, 2 * h:2 * h + 2, :]).then_inc(x_in[k][h], 16)

            load_x(0, 0)
            for kt in range(KT):
                n = S * 2 * P
                sp.dma_start(fwd_sb[:, kt].rearrange("p b c d -> p (b c d)"), fwd[:, kt * n:(kt + 1) * n]
                             ).then_inc(fwd_in[kt], 16)
            load_x(0, 1)
            load_x(1, 0)
            load_x(1, 1)
            sp.dma_start(inv_sb.rearrange("p a b c d -> p (a b c d)"), inv).then_inc(inv_in, 16)
            sp.dma_start(tok_sb[:], tok).then_inc(tok_in, 16)
            sp.dma_start(gw_sb[:], gate_w).then_inc(gate_in, 16)
            sp.dma_start(gb_sb[0:1, :], gate_b.partition_broadcast(1)).then_inc(gate_in, 16)
            sp.dma_start(b1_sb[:], b1.rearrange("e (p c) -> p e c", c=C)).then_inc(b1_in, 16)
            sp.dma_start(b2_sb.rearrange("p e d -> p (e d)"),
                          b2.rearrange("e d -> (e d)").partition_broadcast(P)).then_inc(b2_in, 16)
            sp.dma_start(w1_sb[:], w1.rearrange("e d f -> d e f")).then_inc(w1_in, 16)
            sp.dma_start(w2_sb.rearrange("p e c d -> p e (c d)"),
                         w2.rearrange("e (p c) d -> p e (c d)", c=C)).then_inc(w2_in, 16)
            sp.wait_ge(blank_set, 2)
            sp.dma_start(scratch[BLANK:BLANK + P, :], blank[:]).then_inc(blanks_out, 16)
            blank_tails(sp, range(2))

            def step(t, end):
                load_tile(sp, t)

            all_tiles(sp, step, 0)

        @block.scalar
        def _(act):
            act.dma_start(t_sb.rearrange("p k s d -> p k (s d)"),
                          taps.rearrange("(k p s) d -> p k (s d)", k=BLK, s=S)).then_inc(t_in, 16)
            act.dma_start(misc_sb[:], misc).then_inc(misc_in, 16)
            act.wait_ge(half_set, 1)
            nc.scalar.activation(warm[:, 1:2], half[:, 0:1], ACT.Identity)

            def normalize(src, g, scale, bias):
                nc.scalar.activation(xng[:, g, :], src, ACT.Identity, bias=bias, scale=scale).then_inc(xn_act, 1)

            for n in range(2 * BLK):
                act.wait_ge(nmr_done, n + 1)
                for g in load_groups(n)[:ON_ACT[n]]:
                    normalize(x_group(g), g, rstd[:, g:g + 1], nmr[:, g:g + 1])
                if n == 0:
                    for kt in range(KT):
                        act.wait_ge(t_spec, kt + 1)
                        nc.scalar.activation(ts[:, kt].rearrange("p k r d -> p (k r d)"), ps[:, 6 + kt, :],
                                             ACT.Copy).then_inc(t_copied, 1)
                if n == 1:
                    for kt in range(KT):
                        act.wait_ge(t_copied, kt + 1)
                        nc.scalar.activation(k0i[:, kt, 0, :], ts[:, kt, 0, 1, :], ACT.Copy, scale=-1.0).then_inc(k0_done, 1)
                        nc.scalar.activation(k0i[:, kt, 1, :], ts[:, kt, 0, 1, :], ACT.Copy).then_inc(k0_done, 1)
                    act.wait_ge(misc_in, 16)
                    for kt in range(KT):
                        nc.scalar.activation(t_alt[:, kt, 0:2, :], ts[:, kt, 0], ACT.Copy, scale=alt).then_inc(alt_done, 1)
                        nc.scalar.activation(t_alt[:, kt, 2, :], ts[:, kt, 0, 0, :], ACT.Copy, scale=nalt).then_inc(alt_done, 1)

            def gate_exp(c):
                act.wait_ge(df_done, c + 1)
                nc.scalar.activation(flat(ex[:, c]), flat(df[:, c]), ACT.Exp).then_inc(ex_done, 1)

            act.wait_ge(x_spec, 3 * BLK * KT)
            for c in range(CH):
                act.wait_ge(nmr_done, 2 * BLK + c + 1)
                for g in range(B * c, B * c + ON_ACT2):
                    normalize(rows[:, g, 0:D], g, rows[:, g, RSTD:RSTD + 1], rows[:, g, NMR:NMR + 1])
                if c >= 1:
                    gate_exp(c - 1)
                act.wait_ge(xt_psum, c + 1)
                nc.scalar.activation(xT[:, B * c:B * c + B, :].rearrange("p g d -> p (g d)"),
                                     ps[:, CH + c % 2, :], ACT.Copy).then_inc(xt_done, 1)
            gate_exp(CH - 1)
            nc.scalar.activation(warm[:, 0:1], half[:, 0:1], ACT.Gelu)
            act.wait_ge(blank_set, 2)
            blank_tails(act, range(2, NE))
            act.wait_ge(b1_in, 16)

            def step(t, end):
                par = t % 2
                e = expert_of(act, t)
                act.wait_ge(h_psum, t + 1)
                if t >= 2:
                    act.wait_ge(y_psum, t - 1)
                for c in range(C):
                    nc.scalar.activation(hT[:, par, c, :], ps[:, 2 + par, c * P:(c + 1) * P], ACT.Gelu,
                                         bias=b1_sb[:, bass.ds(e, 1), c]).then_inc(h_done, 1)

            all_tiles(act, step, 0)

        @block.gpsimd
        def _(pool):
            nc.gpsimd.memset(ones_sb[:], 1.0).then_inc(ones_set, 1)
            nc.gpsimd.memset(half[:], -0.5).then_inc(half_set, 1)
            nc.gpsimd.memset(blank[:, 0:TOK], 0.0).then_inc(blank_set, 1)
            nc.gpsimd.memset(blank.bitcast(I32)[:, TOK:TOK + 1], B * N).then_inc(blank_set, 1)
            pool.wait_ge(half_set, 1)

            def inv_sqrt(n, r, v, w, mr):
                pool.wait_ge(var_done, n + 1)
                nc.gpsimd.tensor_tensor(r, v, w, ALU.pow).then_inc(rstd_done, 1)
                pool.wait_ge(rstd_done, n + 1)
                nc.gpsimd.tensor_tensor(mr, mr, r, ALU.mult).then_inc(nmr_done, 1)

            for n in range(2 * BLK):
                inv_sqrt(n, *(halves(a, n // 2, n % 2) for a in (rstd, var, half, nmr)))
            for kt in range(KT):
                pool.wait_ge(alt_done, 2 * kt + 2)
                nc.gpsimd.tensor_tensor(k1r[:, kt, :], ts[:, kt, 1, 0, :], t_alt[:, kt, 1, :], ALU.subtract).then_inc(k1_done, 1)
                nc.gpsimd.tensor_tensor(k1i[:, kt, 0, :], t_alt[:, kt, 2, :], ts[:, kt, 1, 1, :], ALU.subtract).then_inc(k1_done, 1)
                nc.gpsimd.tensor_tensor(k1i[:, kt, 1, :], t_alt[:, kt, 0, :], ts[:, kt, 1, 1, :], ALU.add).then_inc(k1_done, 1)
            pool.wait_ge(tok_in, 16)
            nc.gpsimd.tensor_copy(rows.bitcast(I32)[:, :, TOK], tok_sb[:]).then_inc(tok_set, 1)
            for n, (kt, term) in enumerate(((0, 0), (1, 0), (0, 1), (1, 1))):
                pool.wait_ge(prods, n + 1)
                nc.gpsimd.tensor_tensor(ya[:, kt, term], pr[:, kt, term, 0], pr[:, kt, term, 1], ALU.add
                                        ).then_inc(sums if term else y_spec[kt], 1)
            pool.wait_ge(prods, 5)
            nc.gpsimd.tensor_tensor(pr[:, 0, 2, 0], pr[:, 0, 2, 0], pr[:, 0, 2, 1], ALU.add).then_inc(sums, 1)
            pool.wait_ge(sums, 3)
            nc.gpsimd.tensor_tensor(ya[:, 0, 1], ya[:, 0, 1], pr[:, 0, 2, 0], ALU.add).then_inc(y_spec[0], 1)

            def scatter(g):
                phase = sum(g // B >= c for c, _ in PHASES)
                nc.gpsimd.indirect_dma_start(
                    out=scratch.ap(), out_offset=bass.IndirectOffsetOnAxis(ap=slot[:, g:g + 1], axis=0),
                    in_=rows[:, g, :], in_offset=None).then_inc(rows_out[phase], 16)

            def inv_sqrt_x1(c):
                g0, g1 = B * c, B * c + B
                inv_sqrt(2 * BLK + c, rows[:, g0:g1, RSTD], var[:, g0:g1], half[:, g0:g1], rows[:, g0:g1, NMR])

            inv_sqrt_x1(0)
            inv_sqrt_x1(1)
            inv_sqrt_x1(2)
            pool.wait_ge(tok_set, 1)
            for g in range(G):
                if g % B == 0:
                    pool.wait_ge(slot_done, g // B + 1)
                if g == B // 2:
                    inv_sqrt_x1(3)
                scatter(g)

            def result(t, end):
                pool.wait_ge(o_done, t + 1)
                nc.gpsimd.indirect_dma_start(
                    out=out, out_offset=bass.IndirectOffsetOnAxis(ap=ib[:, t % NOB, :], axis=0),
                    in_=ob[:, t % NOB, :], in_offset=None, bounds_check=B * N - 1, oob_is_err=False
                ).then_inc(o_out[t % NOB], 16)
                if t == end - 1:
                    for n in range(NOB):
                        pool.wait_ge(o_out[n], 16 * len(range(n, end, NOB)))

            all_tiles(pool, result, 0)

        @block.vector
        def _(dve):
            done = [0]

            def link(ins):
                done[0] += 1
                ins.then_inc(dve_step, 1)
                dve.wait_ge(dve_step, done[0])

            def bn(groups, src):
                for g in groups:
                    last = nc.vector.bn_stats(st[:, g, :], src(g))
                return last

            def aggregate(groups, part, mr):
                for g in groups:
                    last = nc.vector.bn_aggr(mv[:, g, :], st[:, g, :])
                link(last)
                nc.vector.tensor_scalar(mr, part(mv[:, :, 0]), -1.0, None, ALU.mult)
                nc.vector.tensor_scalar(part(var), part(mv[:, :, 1]), EPS, None, ALU.add).then_inc(var_done, 1)

            def normalize(g, src, r):
                nc.vector.tensor_scalar(xng[:, g, :], src, mv[:, g, 0:1], r, ALU.subtract, ALU.mult).then_inc(xn_dve, 1)

            def stats_x(n):
                def part(a):
                    return halves(a, n // 2, n % 2)

                dve.wait_ge(x_in[n // 2][n % 2], 16)
                link(bn(load_groups(n), x_group))
                aggregate(load_groups(n), part, part(nmr))

            def normalize_x(n):
                dve.wait_ge(rstd_done, n + 1)
                for g in load_groups(n)[ON_ACT[n]:]:
                    normalize(g, x_group(g), rstd[:, g:g + 1])

            stats_x(0)
            normalize_x(0)
            stats_x(1)
            stats_x(2)
            normalize_x(1)
            stats_x(3)

            def times(kt, term, b0=0, b1=B):
                if term == 2:
                    spec = ps[:, 4 + 2 * kt:6 + 2 * kt, :]
                else:
                    spec = ps[:, b0 + kt, :].rearrange("p (r n) -> p r n", r=2)
                spec = spec.rearrange("p r (b d) -> p r b d", d=D)
                re = k1r[:, kt] if term == 1 else ts[:, kt, 0, 0, :]
                im = k1i[:, kt] if term == 1 else k0i[:, kt]
                to = pr[:, kt, term, :, :, b0 * D:b1 * D].rearrange("p n r (b d) -> p n r b d", d=D)
                nc.vector.tensor_tensor(to[:, 0], spec, re.unsqueeze(1).unsqueeze(1).to_broadcast([P, 2, b1 - b0, D]), ALU.mult)
                return nc.vector.tensor_tensor(to[:, 1], spec[:, ::-1], im.unsqueeze(2).to_broadcast([P, 2, b1 - b0, D]),
                                               ALU.mult)

            for h in range(2):
                for kt in range(KT):
                    dve.wait_ge(k0_done, 2 * kt + 2)
                    dve.wait_ge(x_spec, 4 * h + 2 * kt + 2)
                    last = times(kt, 0, 2 * h, 2 * h + 2)
                    if h:
                        last.then_inc(prods, 1)
                    if h and kt == 0:
                        dve.wait_ge(k1_done, 3)
                        times(0, 1, 0, 2)
            dve.wait_ge(k1_done, 3 * KT)
            times(1, 1, 0, 2)
            for kt in range(KT):
                times(kt, 1, 2, 4).then_inc(prods, 1)
            for kt in range(KT):
                dve.wait_ge(x_spec, 4 * BLK + 2 * kt + 2)
                times(kt, 2).then_inc(prods, 1)
            nc.vector.tensor_copy(oh[:, 0, :, 0], seed).then_inc(seeded, 1)

            def last_spectrum():
                dve.wait_ge(prods, 6)
                link(nc.vector.tensor_tensor(pr[:, 1, 2, 0], pr[:, 1, 2, 0], pr[:, 1, 2, 1], ALU.add))
                dve.wait_ge(sums, 2)
                nc.vector.tensor_tensor(ya[:, 1, 1], ya[:, 1, 1], pr[:, 1, 2, 0], ALU.add).then_inc(y_spec[1], 1)

            def make_x1(c):
                k, s = c // S, c % S
                dve.wait_ge(y_conv, c + 1)
                link(nc.vector.tensor_tensor(rows[:, B * c:B * c + B, 0:D], x_sb[:, k, :, s, :],
                                             ps[:, c, :].rearrange("p (b d) -> p b d", d=D), ALU.add))
                bn(range(B * c, B * c + B), lambda g: rows[:, g, 0:D]).then_inc(bn_done, 1)

            def stats_x1(c):
                g0 = B * c
                dve.wait_ge(bn_done, c + 1)
                aggregate(range(g0, g0 + B), lambda a: a[:, g0:g0 + B], rows[:, g0:g0 + B, NMR])

            def normalize_x1(c):
                dve.wait_ge(rstd_done, 2 * BLK + c + 1)
                for g in range(B * c + ON_ACT2, B * c + B):
                    normalize(g, rows[:, g, 0:D], rows[:, g, RSTD:RSTD + 1])

            def choose(c):
                lg_v = lg_ps[c].rearrange("p (e g) -> p e g", g=B)
                dve.wait_ge(logits, c + 1)
                link(nc.vector.tensor_reduce(red[:, c, 0], by_group(lg_v), AX_X, ALU.max))
                nc.vector.tensor_tensor(df[:, c], lg_v, all_e(red[:, c, 0]), ALU.subtract).then_inc(df_done, 1)
                dve.wait_ge(df_done, c + 1)
                link(nc.vector.scalar_tensor_tensor(flat(sc[:, c]), flat(df[:, c]), 0.0, pick, ALU.is_ge, ALU.mult))
                link(nc.vector.tensor_reduce(red[:, c, 1], by_group(sc[:, c]), AX_X, ALU.max))
                nc.vector.tensor_tensor(oh[:, c, :, 1:], sc[:, c], all_e(red[:, c, 1]), ALU.is_equal).then_inc(oh_done, 1)
                dve.wait_ge(oh_done, c + 1)
                dve.wait_ge(seeded, c + 1)
                nc.vector.tensor_tensor_scan(flat(cum[:, c]), carry, flat(oh[:, c]), 0.0, ALU.mult, ALU.add).then_inc(cum_done, 1)
                dve.wait_ge(cum_done, c + 1)
                nc.vector.tensor_copy(oh[:, c + 1, :, 0], cum[:, c, :, B]).then_inc(seeded, 1)

            def weigh(c):
                dve.wait_ge(ex_done, c + 1)
                link(nc.vector.tensor_reduce(red[:, c, 2], by_group(ex[:, c]), AX_X, ALU.add))
                nc.vector.reciprocal(rows[:, B * c:B * c + B, WGT], red[:, c, 2])

            def place(c):
                dve.wait_ge(ranked, c + 1)
                link(nc.vector.tensor_tensor(pos[:, c], rank_ps[c].rearrange("p (e g) -> p e g", g=B), oh[:, c, :, 1:], ALU.mult))
                link(nc.vector.tensor_reduce(red[:, c, 3], by_group(pos[:, c]), AX_X, ALU.add))
                nc.vector.tensor_copy(slot[:, B * c:B * c + B], red[:, c, 3]).then_inc(slot_done, 1)

            def count(i):
                dve.wait_ge(free_row, i + 1)
                link(nc.vector.tensor_copy(free[:, i], free_ps[i]))
                if i == NP - 1:
                    nc.vector.tensor_copy(freei[0:1, :], free[0:1, i]).then_inc(free_done, 1)

            def plan(i):
                b, br = (base[:, i], base_row[:, i]) if i else (region, tile_row)
                last, n = i == NP - 1, PHASES[i][1]
                end, start, m, taken = (ends[:, i, j] for j in range(4))
                link(nc.vector.tensor_tensor(cnt[:, i], free[:, i], b, ALU.subtract))
                link(nc.vector.tensor_scalar(cnti[:, i, 0], cnt[:, i], float(P - 1 if last else 0), None, ALU.add))
                link(nc.vector.tensor_scalar(cnti[:, i, 1], cnti[:, i, 0], 7, None, ALU.logical_shift_right))
                link(nc.vector.tensor_tensor_scan(end, ones_sb[:, 0:NE], cnti[:, i, 1], 0.0, ALU.mult, ALU.add))
                nc.vector.tensor_scalar(cmp[:, i, 0], end, iota, None, ALU.is_le)
                link(nc.vector.tensor_tensor(start, end, cnti[:, i, 1], ALU.subtract))
                nc.vector.tensor_reduce(ecnt[:, i, 0:1], cmp[:, i, 0], AX_X, ALU.add)
                nc.vector.scalar_tensor_tensor(cmp[:, i, 1], start, iota, cmp[:, i, 0], ALU.is_le, ALU.subtract)
                link(nc.vector.scalar_tensor_tensor(cmp[:, i, 2], start, float(-P), br, ALU.mult, ALU.add))
                if last:
                    nc.vector.tensor_copy(usedi[0:1, :], end[0:1, NE - 1:NE])
                nc.vector.tensor_scalar(eidx[:, i:i + 1], ecnt[:, i, 0:1], float(NE - 1), None, ALU.min).then_inc(eidx_done, 1)
                link(nc.vector.tensor_tensor(cmp[:, i, 3], cmp[:, i, 2], cmp[:, i, 1], ALU.mult))
                link(nc.vector.tensor_reduce(ecnt[:, i, 1:2], cmp[:, i, 3], AX_X, ALU.add))
                nc.vector.tensor_scalar(tfirst[:, i:i + 1], ecnt[:, i, 1:2], float(BLANK), None, ALU.add).then_inc(tfirst_done, 1)
                if not last:
                    link(nc.vector.tensor_scalar(m, start, float(n), None, ALU.min))
                    link(nc.vector.scalar_tensor_tensor(taken, end, float(n), m, ALU.min, ALU.subtract))
                    nc.vector.scalar_tensor_tensor(base[:, i + 1], taken, float(P), b, ALU.mult, ALU.add)
                    link(nc.vector.scalar_tensor_tensor(base_row[:, i + 1], taken, float(P), br, ALU.mult, ALU.add))

            last_spectrum()
            make_x1(0)
            stats_x1(0)
            make_x1(1)
            normalize_x1(0)
            stats_x1(1)
            make_x1(2)
            normalize_x1(1)
            stats_x1(2)
            choose(0)
            normalize_x1(2)
            weigh(0)
            place(0)
            make_x1(3)
            stats_x1(3)
            choose(1)
            normalize_x1(3)
            weigh(1)
            place(1)
            choose(2)
            weigh(2)
            place(2)
            count(0)
            plan(0)
            choose(3)
            weigh(3)
            place(3)
            count(1)
            plan(1)
            dve.wait_ge(w1_in, 16)
            dve.wait_ge(b2_in, 16)

            expert = {}

            def finish(t):
                par = t % NOB
                e = expert[t]
                w = xs[:, t, WGT:WGT + 1]
                nc.vector.scalar_tensor_tensor(yb[:, par % 2, :].unsqueeze(1), b2_sb[:, bass.ds(e, 1), :], w,
                                               xs[:, t, 0:D].unsqueeze(1), ALU.mult, ALU.add).then_inc(yb_done, 1)
                if t >= NOB:
                    dve.wait_ge(o_out[par], 16 * (t // NOB))
                nc.vector.tensor_copy(ib[:, par, :], xs.bitcast(U32)[:, t, TOK:TOK + 1])
                dve.wait_ge(yb_done, t + 1)
                dve.wait_ge(y_psum, t + 1)
                nc.vector.scalar_tensor_tensor(ob[:, par, :], ps[:, 4 + par % 2, 0:D], w, yb[:, par % 2, :],
                                               ALU.mult, ALU.add).then_inc(o_done, 1)

            def hold_w1(u):
                e = expert[u] = expert_of(dve, u)
                if u >= 4:
                    dve.wait_ge(h_psum, u - 3)
                nc.vector.tensor_copy(wst[:, u % 4], w1_sb[:, bass.ds(e, 1), :].rearrange("p e (q c) -> p (e c) q", c=C)
                                      ).then_inc(wst_done, 1)

            def normalize_rows(u):
                dve.wait_ge(xs_in[u], 16)
                if u >= 4:
                    dve.wait_ge(xsT_psum, u - 3)
                nc.vector.tensor_scalar(xsn[:, u % 4, :], xs[:, u, 0:D], xs[:, u, RSTD:RSTD + 1], xs[:, u, NMR:NMR + 1],
                                        ALU.mult, ALU.add).then_inc(xsn_done, 1)

            def transposed(u):
                dve.wait_ge(xsT_psum, u + 1)
                if u >= 4:
                    dve.wait_ge(h_psum, u - 3)
                nc.vector.tensor_copy(xsT[:, u % 4, :], ps[:, u % 2, 0:P]).then_inc(xsT_done, 1)

            def step(t, end):
                if t == -3:
                    for u in range(3):
                        hold_w1(u)
                if 0 <= t < end - 3:
                    hold_w1(t + 3)
                if t == -2:
                    transposed(0)
                    normalize_rows(1)
                else:
                    if t + 3 < end:
                        normalize_rows(t + 3)
                    if 0 <= t + 2 < end:
                        transposed(t + 2)
                if t >= 1:
                    finish(t - 1)

            all_tiles(dve, step, 3, 1)

        @block.tensor
        def _(pe):
            def transform(dst, kt, ri, rhs):
                for s in range(S):
                    last = nc.tensor.matmul(dst, fwd_sb[:, kt, s, ri, :], rhs[s], start=(s == 0), stop=(s == S - 1))
                return last

            pe.wait_ge(ones_set, 1)
            for _ in range(WARM):
                nc.tensor.matmul(ps[:, 0, 0:P], ones_sb[:], ones_sb[:], start=True, stop=True)
            pe.wait_ge(t_in, 16)
            for kt in range(KT):
                pe.wait_ge(fwd_in[kt], 16)
                for k in range(BLK):
                    for ri in range(2):
                        q = (2 * k + ri) * D
                        last = transform(ps[:, 6 + kt, q:q + D], kt, ri, [t_sb[:, k, s, :] for s in range(S)])
                last.then_inc(t_spec, 1)
            for k, b0, b1 in ((0, 0, 2), (0, 2, 4), (1, 0, 4)):
                x_normalized(pe, 2 * k + b1 // 2)
                for kt in range(KT):
                    for ri in range(2):
                        if k:
                            to = ps[:, 4 + 2 * kt + ri, :]
                        else:
                            to = ps[:, b0 + kt, ri * 2 * D:(ri + 1) * 2 * D]
                        if k and kt:
                            pe.wait_ge(t_copied, ri + 1)
                        transform(to, kt, ri, [xn[:, k, s, b0:b1, :] for s in range(S)]
                                  ).then_inc(x_spec, 1)

            def inverse(c, kt):
                k, s = c // S, c % S
                pe.wait_ge(y_spec[kt], k + 1)
                for ri in range(2):
                    last = nc.tensor.matmul(ps[:, c, :], inv_sb[:, kt, ri, s, :], ya[:, kt, k, ri, :],
                                            start=(kt == 0 and ri == 0), stop=(kt == KT - 1 and ri == 1))
                if kt == KT - 1:
                    last.then_inc(y_conv, 1)

            def transposes(c):
                pe.wait_ge(xn_act, sum(ON_ACT) + ON_ACT2 * (c + 1))
                pe.wait_ge(xn_dve, G - sum(ON_ACT) + (B - ON_ACT2) * (c + 1))
                if c >= 2:
                    pe.wait_ge(xt_done, c - 1)
                for b in range(B):
                    last = nc.tensor.transpose(ps[:, CH + c % 2, b * P:(b + 1) * P], xng[:, B * c + b, :], ident)
                last.then_inc(xt_psum, 1)

            def gate_logits(c):
                lg_v = lg_ps[c].rearrange("p (e g) -> p g e", g=B)
                nc.tensor.matmul(lg_v, ones_sb[0:1, :], gb_sb[0:1, :].unsqueeze(1).to_broadcast([1, B, NE]),
                                 start=True, stop=False)
                pe.wait_ge(xt_done, c + 1)
                for b in range(B):
                    last = nc.tensor.matmul(lg_v[:, b, :], xT[:, B * c + b, :], gw_sb[:], start=False, stop=(b == B - 1))
                last.then_inc(logits, 1)

            def keep_warm(n):
                for _ in range(n):
                    nc.tensor.matmul(ps[:, 7, 0:P], ones_sb[:], ones_sb[:], start=True, stop=True)

            def ranks(c):
                rank_v = rank_ps[c].rearrange("p (e g) -> p e g", g=B)
                pe.wait_ge(oh_done, c + 1)
                nc.tensor.matmul(rank_v, rank_w, oh[:, c, :, 1:], start=True, stop=False)
                pe.wait_ge(cum_done, c + 1)
                nc.tensor.matmul(rank_v, ones_sb[:], cum[:, c, :, 1:], start=False, stop=True).then_inc(ranked, 1)
                for i, (chunks, _) in enumerate(PHASES):
                    if chunks == c + 1:
                        nc.tensor.matmul(free_ps[i], ones_sb[:], cum[:, c, :, B], start=True, stop=True).then_inc(free_row, 1)

            pe.wait_ge(inv_in, 16)
            pe.wait_ge(prods, 4)
            for c in range(3):
                for kt in range(KT):
                    inverse(c, kt)
            pe.wait_ge(misc_in, 16)
            pe.wait_ge(gate_in, 32)
            pe.wait_ge(prods, 6)
            transposes(0)
            inverse(3, 0)
            gate_logits(0)
            inverse(3, 1)
            transposes(1)
            ranks(0)
            gate_logits(1)
            transposes(2)
            keep_warm(9)
            ranks(1)
            gate_logits(2)
            transposes(3)
            keep_warm(6)
            ranks(2)
            gate_logits(3)
            keep_warm(14)
            ranks(3)

            pe.wait_ge(w2_in, 16)
            pe.wait_ge(free_done, 1)
            keep_warm(22)

            def transpose_rows(u):
                pe.wait_ge(xsn_done, u + 1)
                if u >= 2:
                    pe.wait_ge(xsT_done, u - 1)
                nc.tensor.transpose(ps[:, u % 2, 0:P], xsn[:, u % 4, :], ident).then_inc(xsT_psum, 1)

            def hidden(u):
                pe.wait_ge(xsT_done, u + 1)
                pe.wait_ge(wst_done, u + 1)
                if u >= 2:
                    pe.wait_ge(h_done, C * (u - 1))
                for c in range(C):
                    last = nc.tensor.matmul(ps[:, 2 + u % 2, c * P:(c + 1) * P], wst[:, u % 4, c, :], xsT[:, u % 4, :],
                                            start=True, stop=True)
                last.then_inc(h_psum, 1)

            def project(t):
                e = expert_of(pe, t)
                if t >= 2:
                    pe.wait_ge(o_done, t - 1)
                for c in range(C):
                    pe.wait_ge(h_done, C * t + c + 1)
                    last = nc.tensor.matmul(ps[:, 4 + t % 2, 0:D], hT[:, t % 2, c, :], w2_sb[:, bass.ds(e, 1), c, :],
                                            start=(c == 0), stop=(c == C - 1))
                last.then_inc(y_psum, 1)

            def step(t, end):
                if t == -1:
                    hidden(0)
                    transpose_rows(1)
                else:
                    if t + 2 < end:
                        transpose_rows(t + 2)
                    if 0 <= t + 1 < end:
                        hidden(t + 1)
                if t >= 0:
                    project(t)

            all_tiles(pe, step, 2)


_INS = ['L0_attn_x', 'L0_attn_t', 'L0_ffn_gate_w', 'L0_ffn_gate_b', 'L0_ffn_w1', 'L0_ffn_b1', 'L0_ffn_w2', 'L0_ffn_b2']


def _constants(np):
    L = 2 * N // BLK
    k = np.arange(L // 2)
    n = np.arange(N // BLK)
    th = 2 * np.pi * np.outer(n, k + 0.5) / L
    f = np.stack([np.cos(th), -np.sin(th)], 1)
    fwd = f.reshape(P, S, 2, KT, P).transpose(0, 3, 1, 2, 4)
    inv = (f * (2.0 / L)).reshape(P, S, 2, KT, P).transpose(4, 3, 2, 1, 0)
    misc = np.zeros((P, M_COLS))
    misc[:, M_ID:M_ID + P] = np.eye(P)
    misc[:, M_RANK:M_RANK + P] = np.triu(np.ones((P, P)), 1) - 1
    misc[:, M_ALT] = 1 - 2 * (np.arange(P) % 2)
    misc[:, M_ALT + 1] = -misc[:, M_ALT]
    misc[:, M_PICK:M_CARRY] = np.repeat(np.arange(NE, 0, -1), B)
    misc[:, M_CARRY:M_IOTA] = np.tile(np.arange(B + 1) > 0, NE)
    misc[:, M_IOTA] = np.arange(P)
    misc[:, M_REG:M_SEED] = np.arange(NE) * REGION
    misc[:, M_SEED:M_FIRST] = np.arange(NE) * (REGION // P)
    misc[:, M_FIRST:] = np.arange(NE) * REGION - BLANK + P * np.arange(P)[:, None]
    kk, ss, bb = np.meshgrid(np.arange(BLK), np.arange(S), np.arange(B), indexing="ij")
    tok = (bb * N + kk * (N // BLK) + ss).reshape(1, G) + S * np.arange(P)[:, None]
    return (fwd.reshape(P, -1).astype(np.float32), inv.reshape(P, -1).astype(np.float32),
            misc.astype(np.float32), tok.astype(np.int32))


def kernel(**inputs):
    import numpy as _np
    import concourse.bacc as _bacc
    from concourse import mybir as _mybir
    from concourse.bass_utils import run_bass_kernel_spmd as _run

    nc = _bacc.Bacc("TRN2", target_bir_lowering=False, num_devices=1)
    arrays, args = {}, []
    named = [(n, _np.ascontiguousarray(inputs[n])) for n in _INS]
    named += list(zip(("fwd", "inv", "misc", "tok"), map(_np.ascontiguousarray, _constants(_np))))
    for name, a in named:
        arrays[f"in_{name}_dram"] = a
        args.append(nc.dram_tensor(f"in_{name}_dram", a.shape, _mybir.dt.from_np(a.dtype), kind="ExternalInput").ap())
    out = nc.dram_tensor("out_0_dram", (B * N, D), _mybir.dt.float32, kind="ExternalOutput").ap()
    build(nc, *args, out)
    r = _run(nc, [arrays], core_ids=[0])
    return r.results[0]["out_0_dram"].reshape(B, N, D)
```
